# Optimizing a Trainium2 kernel written in Bass

```python
import numpy as np
import jax
import jax.numpy as jnp

def _softmax(x, axis=-1):
    return jax.nn.softmax(x, axis=axis)

def _gelu(x):
    return jax.nn.gelu(x, approximate=True)

def _silu(x):
    return jax.nn.silu(x)

def _sigmoid(x):
    return jax.nn.sigmoid(x)

def _layernorm(x, axis=-1, eps=1e-05):
    m = jnp.mean(x, axis=axis, keepdims=True)
    v = jnp.var(x, axis=axis, keepdims=True)
    return (x - m) / jnp.sqrt(v + eps)

def _scatter_add(tgt, idx, src, axis=0):
    return tgt.at[idx].add(src)

def _segment_sum(src, seg, n):
    return jax.ops.segment_sum(src, seg, n)
kernel_name = 'mk_adaln_d1_jaxref_r8_c41acb'

def setup_inputs(seed: int=0):
    np.random.seed(seed)
    _w = jnp.asarray

    def _L0_attn_setup():
        import jax, jax.numpy as jnp
        import numpy as np
        D = 128
        key = jax.random.key(seed)
        k0, k1, k2, k3 = jax.random.split(key, 4)
        x = jax.random.normal(k0, (4, 256, D), dtype=jnp.float32)
        Wk = jax.random.normal(k1, (D, D), dtype=jnp.float32) * 0.02
        Wq = jax.random.normal(k2, (D, D), dtype=jnp.float32) * 0.02
        Wv = jax.random.normal(k3, (D, D), dtype=jnp.float32) * 0.02
        return {'x': x, 'Wk': Wk, 'Wq': Wq, 'Wv': Wv}
    _L0_attn_in = _L0_attn_setup()

    def _L0_ffn_setup():
        import jax, jax.numpy as jnp
        import numpy as np
        from jax import lax
        HIDDEN = 128
        INTER = 64
        E = 64
        K = 6
        G = 8
        TG = 4
        NSH = 2
        ISH = INTER * NSH

        def _moe_forward(hidden_states, gate_w, gate_bias, eg_w, eu_w, ed_w, sg_w, su_w, sd_w):
            B, S, H = hidden_states.shape
            x = hidden_states.reshape(-1, H)
            T = x.shape[0]
            shared = jax.nn.silu(x @ sg_w.T) * (x @ su_w.T) @ sd_w.T
            logits = x @ gate_w.T
            scores = jax.nn.sigmoid(logits) + gate_bias
            group_scores = scores.reshape(T, G, E // G).max(axis=-1)
            _, sel_groups = lax.top_k(group_scores, TG)
            group_mask = jnp.zeros((T, G), scores.dtype).at[jnp.arange(T)[:, None], sel_groups].set(1.0)
            mask = jnp.repeat(group_mask, E // G, axis=1)
            masked_scores = scores * mask
            topk_w, topk_i = lax.top_k(masked_scores, K)
            topk_w = topk_w / (topk_w.sum(axis=-1, keepdims=True) + 1e-08)
            comb = jnp.zeros((T, E), x.dtype).at[jnp.arange(T)[:, None], topk_i].add(topk_w)
            h = jax.nn.silu(jnp.einsum('th,eih->eti', x, eg_w)) * jnp.einsum('th,eih->eti', x, eu_w)
            routed = jnp.einsum('eti,ehi,te->th', h, ed_w, comb)
            return (shared + routed).reshape(B, S, H)
        key = jax.random.key(seed)
        ks = jax.random.split(key, 9)
        s = 0.02
        return {'hidden_states': jax.random.normal(ks[0], (1, 128, HIDDEN), jnp.float32), 'gate_w': jax.random.normal(ks[1], (E, HIDDEN), jnp.float32) * s, 'gate_bias': jnp.zeros((E,), jnp.float32), 'eg_w': jax.random.normal(ks[2], (E, INTER, HIDDEN), jnp.float32) * s, 'eu_w': jax.random.normal(ks[3], (E, INTER, HIDDEN), jnp.float32) * s, 'ed_w': jax.random.normal(ks[4], (E, HIDDEN, INTER), jnp.float32) * s, 'sg_w': jax.random.normal(ks[5], (ISH, HIDDEN), jnp.float32) * s, 'su_w': jax.random.normal(ks[6], (ISH, HIDDEN), jnp.float32) * s, 'sd_w': jax.random.normal(ks[7], (HIDDEN, ISH), jnp.float32) * s}
    _L0_ffn_in = _L0_ffn_setup()
    _L0_c = _w((lambda *s: np.random.randn(*s).astype(np.float32) * 0.05)(16, 128))
    _L0_wmod = _w((lambda *s: np.random.randn(*s).astype(np.float32) * 0.05)(128, 6 * 128) * 128 ** (-0.5))
    _d = {'L0_attn_x': _L0_attn_in['x'], 'L0_attn_Wk': _L0_attn_in['Wk'], 'L0_attn_Wq': _L0_attn_in['Wq'], 'L0_attn_Wv': _L0_attn_in['Wv'], 'L0_ffn_gate_w': _L0_ffn_in['gate_w'], 'L0_ffn_gate_bias': _L0_ffn_in['gate_bias'], 'L0_ffn_eg_w': _L0_ffn_in['eg_w'], 'L0_ffn_eu_w': _L0_ffn_in['eu_w'], 'L0_ffn_ed_w': _L0_ffn_in['ed_w'], 'L0_ffn_sg_w': _L0_ffn_in['sg_w'], 'L0_ffn_su_w': _L0_ffn_in['su_w'], 'L0_ffn_sd_w': _L0_ffn_in['sd_w'], 'L0_c': _L0_c, 'L0_wmod': _L0_wmod}
    _x0 = _d['L0_attn_x']
    _d['L0_attn_x'] = jax.random.normal(jax.random.fold_in(jax.random.key(seed), 1), (16, 256, 128), dtype=_x0.dtype)
    del _x0
    return _d

def reference(L0_attn_x, L0_attn_Wk, L0_attn_Wq, L0_attn_Wv, L0_ffn_gate_w, L0_ffn_gate_bias, L0_ffn_eg_w, L0_ffn_eu_w, L0_ffn_ed_w, L0_ffn_sg_w, L0_ffn_su_w, L0_ffn_sd_w, L0_c, L0_wmod):

    def _L0_attn_ref(x, Wk, Wq, Wv):
        import jax, jax.numpy as jnp
        import numpy as np
        D = 128
        K = x @ Wk
        Q = x @ Wq
        V = x @ Wv
        N = Q.shape[-2]
        d = K.shape[-1]
        scores = jnp.einsum('bnd,bmd->bnm', Q, K) / jnp.sqrt(jnp.float32(d))
        causal = jnp.tril(jnp.ones((N, N), dtype=bool))
        scores = jnp.where(causal[None, :, :], scores, -jnp.inf)
        attn = jax.nn.softmax(scores, axis=-1)
        return attn @ V

    def _L0_ffn_ref(hidden_states, gate_w, gate_bias, eg_w, eu_w, ed_w, sg_w, su_w, sd_w):
        import jax, jax.numpy as jnp
        import numpy as np
        from jax import lax
        HIDDEN = 128
        INTER = 64
        E = 64
        K = 6
        G = 8
        TG = 4
        NSH = 2
        ISH = INTER * NSH

        def _moe_forward(hidden_states, gate_w, gate_bias, eg_w, eu_w, ed_w, sg_w, su_w, sd_w):
            B, S, H = hidden_states.shape
            x = hidden_states.reshape(-1, H)
            T = x.shape[0]
            shared = jax.nn.silu(x @ sg_w.T) * (x @ su_w.T) @ sd_w.T
            logits = x @ gate_w.T
            scores = jax.nn.sigmoid(logits) + gate_bias
            group_scores = scores.reshape(T, G, E // G).max(axis=-1)
            _, sel_groups = lax.top_k(group_scores, TG)
            group_mask = jnp.zeros((T, G), scores.dtype).at[jnp.arange(T)[:, None], sel_groups].set(1.0)
            mask = jnp.repeat(group_mask, E // G, axis=1)
            masked_scores = scores * mask
            topk_w, topk_i = lax.top_k(masked_scores, K)
            topk_w = topk_w / (topk_w.sum(axis=-1, keepdims=True) + 1e-08)
            comb = jnp.zeros((T, E), x.dtype).at[jnp.arange(T)[:, None], topk_i].add(topk_w)
            h = jax.nn.silu(jnp.einsum('th,eih->eti', x, eg_w)) * jnp.einsum('th,eih->eti', x, eu_w)
            routed = jnp.einsum('eti,ehi,te->th', h, ed_w, comb)
            return (shared + routed).reshape(B, S, H)
        return _moe_forward(hidden_states, gate_w, gate_bias, eg_w, eu_w, ed_w, sg_w, su_w, sd_w)
    x = L0_attn_x
    mod = (_silu(L0_c) @ L0_wmod).reshape(L0_c.shape[0], 6, 1, -1)
    sa, ca, ga, sb, cb, gb = (mod[:, 0], mod[:, 1], mod[:, 2], mod[:, 3], mod[:, 4], mod[:, 5])
    ga = (2 * (ga >= 0) - 1) * jnp.maximum(jnp.abs(ga), 0.25)
    gb = (2 * (gb >= 0) - 1) * jnp.maximum(jnp.abs(gb), 0.25)
    h = _layernorm(x, axis=-1) * (1 + ca) + sa
    x = x + ga * _L0_attn_ref(h, L0_attn_Wk, L0_attn_Wq, L0_attn_Wv)
    h = _layernorm(x, axis=-1) * (1 + cb) + sb
    x = x + gb * _L0_ffn_ref(h, L0_ffn_gate_w, L0_ffn_gate_bias, L0_ffn_eg_w, L0_ffn_eu_w, L0_ffn_ed_w, L0_ffn_sg_w, L0_ffn_su_w, L0_ffn_sd_w)
    return x

_drawn_inputs = setup_inputs


def setup_inputs(seed=0):
    import zlib

    import numpy as np

    out = dict(_drawn_inputs(seed))
    spreads = {'L0_ffn_gate_bias': (0.0, 0.8)}
    factors = {'L0_attn_Wk': 8.0,
     'L0_attn_Wq': 8.0,
     'L0_attn_Wv': 6.465,
     'L0_ffn_gate_w': 8.0,
     'L0_ffn_eg_w': 8.0,
     'L0_ffn_eu_w': 8.0,
     'L0_ffn_ed_w': 8.0,
     'L0_ffn_sg_w': 8.0,
     'L0_ffn_su_w': 8.0,
     'L0_ffn_sd_w': 8.0,
     'L0_c': 6.448,
     'L0_wmod': 6.337}
    for name, (base, spread) in spreads.items():
        noise = np.random.default_rng([zlib.crc32(name.encode()), seed]).standard_normal(out[name].shape)
        drawn = base * np.exp(spread * noise) if base else spread * noise
        out[name] = jnp.asarray(drawn.astype(out[name].dtype))
    for name, factor in factors.items():
        out[name] = (out[name] * factor).astype(out[name].dtype)
    return out
```

```python
from contextlib import ExitStack

import concourse.bass as bass
from concourse import mybir

F32 = mybir.dt.float32
I32 = mybir.dt.int32
ALU = mybir.AluOpType
ACT = mybir.ActivationFunctionType
AX_X = mybir.AxisListType.X

P = 128
BATCH, SEQ, D = 16, 256, 128
TOKENS = BATCH * SEQ
CT = 512
NC_ = TOKENS // CT
TPC = CT // P
BPC = CT // SEQ
E, INTER, GROUPS, TOPG, TOPK = 64, 64, 8, 4, 6
GE = E // GROUPS
NSH = 2
EA = E + NSH
QUAD = 4
LIST = -(-EA // QUAD) * QUAD
NMOD = 6
SA, CA, GA, SB, CB, GB = range(NMOD)
SW = P + SEQ
EPS = 1e-5
BIG = 1e30


def build(nc, x, cT, wmod, wqT, wkT, wv, gate_wT, gate_bias, w_gu, w_down, comb_dram, out):
    with ExitStack() as ctx:
        def sb(name, shape, dt=F32):
            return ctx.enter_context(nc.sbuf_tensor(name, shape, dt))

        def sem(name):
            return ctx.enter_context(nc.semaphore(name))

        bank = [ctx.enter_context(nc.psum_tensor(f"bank{i}", [P, 512], F32)) for i in range(8)]

        ident = sb("ident", [P, P])
        causal = sb("causal", [P, P])
        tri = sb("tri", [EA, EA])
        place_no = sb("place_no", [P, LIST])
        expert_no = sb("expert_no", [P, 1])
        ones = sb("ones", [P, 1])
        quad_start = sb("quad_start", [1, LIST // QUAD])
        seg_e = sb("seg_e", [P, TPC, E])
        seg_g = sb("seg_g", [P, TPC, GROUPS])
        half_neg = sb("half_neg", [P, TPC])
        cT_sb = sb("cT_sb", [P, BATCH])
        silu_c = sb("silu_c", [P, BATCH])
        mod_tmp = sb("mod_tmp", [P, 2, D])
        wmod_sb = sb("wmod_sb", [P, NMOD * D])
        wqT_sb = sb("wqT_sb", [P, D])
        wkT_sb = sb("wkT_sb", [P, D])
        wv_sb = sb("wv_sb", [P, D])
        wqk = sb("wqk", [P, D])
        gate_sb = sb("gate_sb", [P, E])
        bias_sb = sb("bias_sb", [P, E])
        modT = sb("modT", [P, NMOD, BATCH])
        ga_row = sb("ga_row", [BATCH, D])
        ga_all = sb("ga_all", [P, BATCH, D])

        x_all = sb("x_all", [P, TPC * NC_, D])
        stats = [sb(f"stats{n}", [P, TPC, 6]) for n in (1, 2)]
        mv = [sb(f"mean_var{n}", [P, TPC, 2]) for n in (1, 2)]
        veps = [sb(f"var_eps{n}", [P, TPC]) for n in (1, 2)]
        rstd = [sb(f"rstd{n}", [P, TPC]) for n in (1, 2)]
        xn = [sb(f"xn{n}", [P, TPC, D]) for n in (1, 2)]
        hT = sb("hT", [P, CT])
        gT = sb("gT", [P, CT])
        v_sb = sb("v_sb", [P, TPC, D])
        neg_max = sb("neg_max", [P, TPC])
        sums = sb("sums", [P, TPC])
        rsum = sb("rsum", [P, TPC])
        probs = sb("probs", [P, BPC, SW])
        probsT = sb("probsT", [P, BPC, SW])
        h2T = sb("h2T", [P, TOKENS])
        score = sb("score", [P, TPC, E])
        grp = sb("grp", [P, TPC, GROUPS])
        grp_top = sb("grp_top", [P, TPC, 8])
        grp_gt = sb("grp_gt", [P, TPC, GROUPS])
        grp_eq = sb("grp_eq", [P, TPC, GROUPS])
        grp_run = sb("grp_run", [P, TPC, GROUPS])
        masked = sb("masked", [P, TPC, E])
        top = sb("top", [P, TPC, 8])
        top_gt = sb("top_gt", [P, TPC, 8])
        cnt = sb("cnt", [P, TPC])
        e_gt = sb("e_gt", [P, TPC, E])
        e_eq = sb("e_eq", [P, TPC, E])
        e_run = sb("e_run", [P, TPC, E])
        wsum = sb("wsum", [P, TPC])
        comb = sb("comb", [P, TPC, EA])
        combT = sb("combT", [EA, NC_, CT])
        act_max = sb("act_max", [EA, NC_])
        act = sb("act", [EA, NC_])
        pos = sb("pos", [EA, NC_])
        onehot = sb("onehot", [EA, NC_, LIST])
        comb_list = sb("comb_list", [LIST, 2, CT])
        lists = sb("lists", [1, NC_ * LIST], I32)
        before = sb("before", [1, NC_, LIST // QUAD])
        n_iter = sb("n_iter", [1, NC_])
        zero8 = sb("zero8", [1, NC_])
        iter_f = sb("iter_f", [1, NC_ + 1])
        iter_at = sb("iter_at", [1, NC_ + 1], I32)
        iter_last = sb("iter_last", [1, NC_], I32)

        gu = [sb(f"gu_{u}", [P, 2, 2 * INTER]) for u in "ab"]
        wd = [sb(f"wd_{u}", [P, D]) for u in "ab"]
        comb_b = [sb(f"comb_{u}", [P, CT]) for u in "ab"]
        silu = [sb(f"silu_{u}", [P, CT]) for u in "ab"]
        act_g = [sb(f"weighted_{u}", [P, CT]) for u in "ab"]
        act_h = [sb(f"hidden_{u}", [P, CT]) for u in "ab"]
        zeros = sb("zeros", [P, P])
        yT = [sb(f"yT{n}", [P, CT]) for n in range(2)]
        y = [sb(f"y{n}", [P, TPC, D]) for n in range(2)]

        weights_in = sem("weights_in")
        x_in = [sem(f"x_in{c}") for c in range(NC_)]
        consts_done = sem("consts_done")
        pool_step = sem("pool_step")
        dve_step = sem("dve_step")
        act_step = sem("act_step")
        expc_done = sem("expc_done")
        siluc_done = sem("siluc_done")
        mod_mm = sem("mod_mm")
        mod_ready = sem("mod_ready")
        gab_mm = sem("gab_mm")
        gab_ready = sem("gab_ready")
        wqk_ready = sem("wqk_ready")
        var_done = [sem(f"var{n}_done") for n in (1, 2)]
        rstd_done = [sem(f"rstd{n}_done") for n in (1, 2)]
        xn_done = [sem(f"xn{n}_done") for n in (1, 2)]
        xnT_done = [sem(f"xnT{n}_done") for n in (1, 2)]
        hT_done = sem("hT_done")
        g_mm = sem("g_mm")
        gT_done = sem("gT_done")
        v_mm = sem("v_mm")
        v_done = sem("v_done")
        s_mm = sem("s_mm")
        max_done = sem("max_done")
        probs_done = sem("probs_done")
        pT_mm = sem("pT_mm")
        pT_done = sem("pT_done")
        o_mm = sem("o_mm")
        x2_done = sem("x2_done")
        h2T_done = sem("h2T_done")
        logit_mm = sem("logit_mm")
        logit_exp = sem("logit_exp")
        comb_done = sem("comb_done")
        combT_mm = sem("combT_mm")
        combT_done = sem("combT_done")
        act_max_done = sem("act_max_done")
        act_done = sem("act_done")
        pos_mm = sem("pos_mm")
        onehot_done = sem("onehot_done")
        list_mm = sem("list_mm")
        comb_list_mm = sem("comb_list_mm")
        comb_list_done = sem("comb_list_done")
        comb_out = [sem(f"comb_out{n}") for n in range(2)]
        tables_done = sem("tables_done")

        gu_in = [sem(f"gu_in_{u}") for u in "ab"]
        wd_in = [sem(f"wd_in_{u}") for u in "ab"]
        comb_in = [sem(f"comb_in_{u}") for u in "ab"]
        gate_mm = [sem(f"gate_mm_{u}") for u in "ab"]
        up_mm = [sem(f"up_mm_{u}") for u in "ab"]
        silu_done = [sem(f"silu_done_{u}") for u in "ab"]
        weighted_done = [sem(f"weighted_done_{u}") for u in "ab"]
        hidden_done = [sem(f"hidden_done_{u}") for u in "ab"]
        down_mm = [sem(f"down_mm_{u}") for u in "ab"]
        y_mm = [sem(f"y_mm{n}") for n in range(2)]
        yT_done = [sem(f"yT_done{n}") for n in range(2)]
        yT_mm = [sem(f"yT_mm{n}") for n in range(2)]
        y_done = [sem(f"y_done{n}") for n in range(2)]
        y_out = [sem(f"y_out{n}") for n in range(2)]

        x_v = x.rearrange("b (s p) d -> p (b s) d", p=P)
        out_v = out.rearrange("b (s p) d -> p (b s) d", p=P)
        gate_ps = [bank[0], bank[2]]
        up_ps = [bank[1], bank[3]]
        out_ps = [bank[4], bank[5]]
        t_ps = [bank[6], bank[7]]

        def tiles(c):
            return slice(TPC * c, TPC * (c + 1))

        def wait(eng, s, n):
            if n > 0:
                eng.wait_ge(s, n)

        block = ctx.enter_context(nc.Block())

        @block.sync
        def _(sp):
            for dst, src in ((cT_sb[:], cT), (wqT_sb[:], wqT), (wkT_sb[:], wkT), (wmod_sb[:], wmod),
                             (wv_sb[:], wv), (gate_sb[:], gate_wT),
                             (bias_sb[:], gate_bias.partition_broadcast(P))):
                sp.dma_start(dst, src).then_inc(weights_in, 16)
            for c in range(NC_):
                sp.dma_start(x_all[:, tiles(c), :], x_v[:, tiles(c), :]).then_inc(x_in[c], 16)
            for c in range(NC_):
                sp.wait_ge(comb_list_done, c + 1)
                sp.dma_start(comb_dram[c * LIST:(c + 1) * LIST, :],
                             comb_list[:, c % 2, :]).then_inc(comb_out[c % 2], 16)
            sp.wait_ge(tables_done, 1)
            for half in range(2):
                sp.wait_ge(comb_out[half], 16 * NC_ // 2)

            def load_quads(c, lo, hi):
                with sp.Fori(lo, hi) as i:
                    at = nc.s_assert_within(sp.snap(c * LIST + (i - lo) * QUAD), 0, NC_ * LIST - QUAD, skip_runtime_bounds_check_because="a chunk has at most LIST places")
                    for u in range(2):
                        sp.wait_ge(up_mm[u], i)
                        who = [sp.value_load(lists[0:1, bass.ds(at + 2 * u + k, 1)], min_val=0, max_val=EA - 1)
                               for k in range(2)]
                        for k in range(2):
                            sp.dma_start(gu[u][:, :, INTER * k:INTER * (k + 1)],
                                         w_gu[bass.ds(who[k], 1)].rearrange("e p (h n) -> (e p) h n", h=2)
                                         ).then_inc(gu_in[u], 16)
                        sp.wait_ge(down_mm[u], i)
                        for k in range(2):
                            sp.dma_start(wd[u][INTER * k:INTER * (k + 1), :],
                                         w_down[bass.ds(who[k], 1)].rearrange("e p n -> (e p) n")
                                         ).then_inc(wd_in[u], 16)

            def load_chunk(c):
                lo = sp.value_load(iter_at[0:1, bass.ds(c, 1)], min_val=1, max_val=NC_ * LIST)
                hi = sp.value_load(iter_at[0:1, bass.ds(c + 1, 1)], min_val=1, max_val=NC_ * LIST)
                load_quads(c, lo, hi)

            def store_chunk(n1, par):
                sp.wait_ge(y_done[par], n1 + 1)
                sp.dma_start(out_v[:, bass.ds(2 * TPC * n1 + TPC * (par - 2), TPC), :], y[par][:]
                             ).then_inc(y_out[par], 16)

            for par in range(2):
                load_chunk(par)
            with sp.Fori(1, NC_ // 2) as n:
                for par in range(2):
                    load_chunk(2 * n + par)
                    store_chunk(n, par)
            for par in range(2):
                store_chunk(NC_ // 2, par)
            for par in range(2):
                sp.wait_ge(y_out[par], 16 * NC_ // 2)

        @block.gpsimd
        def _(pool):
            n = [0]

            def link(ins):
                n[0] += 1
                ins.then_inc(pool_step, 1)
                pool.wait_ge(pool_step, n[0])

            link(nc.gpsimd.memset(ident[:], 0.0))
            link(nc.gpsimd.memset(causal[:], 0.0))
            link(nc.gpsimd.memset(tri[:], 1.0))
            nc.gpsimd.affine_select(out=ident[:], in_=ident[:], compare_op=ALU.not_equal, fill=1.0,
                                    base=0, pattern=[[-1, P]], channel_multiplier=1).then_inc(consts_done, 1)
            nc.gpsimd.affine_select(out=causal[:], in_=causal[:], compare_op=ALU.is_ge, fill=-BIG,
                                    base=0, pattern=[[-1, P]], channel_multiplier=1).then_inc(consts_done, 1)
            nc.gpsimd.affine_select(out=tri[:], in_=tri[:], compare_op=ALU.is_gt, fill=0.0,
                                    base=0, pattern=[[1, EA]], channel_multiplier=-1).then_inc(consts_done, 1)
            nc.gpsimd.iota(place_no[:], pattern=[[1, LIST]], base=0, channel_multiplier=0,
                           allow_small_or_imprecise_dtypes=True).then_inc(consts_done, 1)
            nc.gpsimd.iota(expert_no[:], pattern=[[0, 1]], base=0, channel_multiplier=1,
                           allow_small_or_imprecise_dtypes=True).then_inc(consts_done, 1)
            nc.gpsimd.iota(quad_start[:], pattern=[[QUAD, LIST // QUAD]], base=0, channel_multiplier=0,
                           allow_small_or_imprecise_dtypes=True).then_inc(consts_done, 1)
            link(nc.gpsimd.memset(half_neg[:], -0.5))

            def deviation(k, c):
                pool.wait_ge(var_done[k], c + 1)
                nc.gpsimd.tensor_tensor(rstd[k][:], veps[k][:], half_neg[:], ALU.pow).then_inc(rstd_done[k], 1)

            for c in range(NC_ + 1):
                if c < NC_:
                    deviation(0, c)
                if c >= 1:
                    deviation(1, c - 1)

            pool.wait_ge(tables_done, 1)
            for u in range(2):
                nc.gpsimd.memset(act_g[u][:, 0:1], 0.0).then_inc(weighted_done[u], 1)
            with pool.Fori(0, NC_) as c:
                lo = pool.value_load(iter_at[0:1, bass.ds(c, 1)], min_val=1, max_val=NC_ * LIST)
                hi = pool.value_load(iter_at[0:1, bass.ds(c + 1, 1)], min_val=1, max_val=NC_ * LIST)
                with pool.Fori(lo, hi) as i:
                    for u in range(2):
                        pool.wait_ge(silu_done[u], i + 1)
                        pool.wait_ge(comb_in[u], i * 32)
                        pool.wait_ge(hidden_done[u], i)
                        nc.gpsimd.tensor_tensor(act_g[u][:], silu[u][:], comb_b[u][:],
                                                ALU.mult).then_inc(weighted_done[u], 1)

        @block.scalar
        def _(act_e):
            act_e.wait_ge(weights_in, 16 * 7)
            nc.scalar.activation(silu_c[:], cT_sb[:], ACT.Exp, scale=-1.0).then_inc(expc_done, 1)
            act_e.wait_ge(mod_mm, 1)
            nc.scalar.activation(wqk[:], bank[0][:, 0:D], ACT.Copy, scale=float(D) ** -0.5).then_inc(wqk_ready, 1)
            for n in range(BATCH // 4):
                act_e.wait_ge(gab_mm, n + 1)
                nc.scalar.copy(ga_all[:, 4 * n:4 * n + 4, :].rearrange("p b d -> p (b d)"),
                               bank[3 + n][:]).then_inc(gab_ready, 1)

            def modulate(dst, k, src, shift, scale, c, done):
                for q in range(BPC):
                    b = BPC * c + q
                    w = slice(SEQ * q, SEQ * (q + 1))
                    ins = nc.scalar.activation(dst[:, w], src[:, w], ACT.Identity,
                                               bias=modT[:, shift, b:b + 1], scale=modT[:, scale, b:b + 1])
                ins.then_inc(done, 1)

            def attend_a(c):
                act_e.wait_ge(xnT_done[0], c + 1)
                wait(act_e, s_mm, BPC * c)
                if c == 0:
                    act_e.wait_ge(mod_ready, 1)
                modulate(hT, 0, bank[0], SA, CA, c, hT_done)
                act_e.wait_ge(g_mm, c + 1)
                nc.scalar.copy(gT[:], bank[1][:]).then_inc(gT_done, 1)

            def attend_b(c):
                for q in range(BPC):
                    act_e.wait_ge(max_done, BPC * c + q + 1)
                    wait(act_e, pT_mm, BPC * (c - 1) + q + 1)
                    wait(act_e, x2_done, c)
                    for r, w in enumerate((slice(0, P), slice(P, SW))):
                        ins = nc.scalar.activation(probs[:, q, w], bank[3 + q][:, w], ACT.Exp,
                                                   bias=neg_max[:, 2 * q + r:2 * q + r + 1],
                                                   accum_out=sums[:, 2 * q + r:2 * q + r + 1])
                    ins.then_inc(probs_done, 1)
                for q in range(BPC):
                    act_e.wait_ge(pT_mm, BPC * c + q + 1)
                    wait(act_e, o_mm, c)
                    nc.scalar.copy(probsT[:, q, :], bank[q][:, 0:SW]).then_inc(pT_done, 1)

            def route_a(c):
                act_e.wait_ge(xnT_done[1], c + 1)
                modulate(h2T[:, c * CT:(c + 1) * CT], 1, bank[5], SB, CB, c, h2T_done)

            def route_b(c):
                act_e.wait_ge(logit_mm, c + 1)
                wait(act_e, comb_done, c)
                nc.scalar.activation(score[:].rearrange("p t e -> p (t e)"), bank[6][:, 0:TPC * E], ACT.Exp,
                                     scale=-1.0).then_inc(logit_exp, 1)

            def route_c(c):
                act_e.wait_ge(combT_mm, c + 1)
                nc.scalar.copy(combT[:, c, :], bank[7][0:EA, :]).then_inc(combT_done, 1)

            for c in range(NC_ + 1):
                if c < NC_:
                    attend_a(c)
                if c >= 1:
                    route_a(c - 1)
                    route_b(c - 1)
                if c < NC_:
                    attend_b(c)
                if c >= 1:
                    route_c(c - 1)

            for c in range(NC_):
                act_e.wait_ge(comb_list_mm, c + 1)
                wait(act_e, comb_out[c % 2], 16 * (c // 2))
                nc.scalar.copy(comb_list[:, c % 2, :], bank[c % 2][0:LIST, :]).then_inc(comb_list_done, 1)

            act_e.wait_ge(tables_done, 1)
            for half in range(2):
                act_e.wait_ge(comb_out[half], 16 * NC_ // 2)
            for u in range(2):
                nc.scalar.activation(silu[u][:, 0:1], ones[:], ACT.Silu).then_inc(silu_done[u], 1)
            for par in range(2):
                nc.scalar.copy(yT[par][:, 0:1], ones[:]).then_inc(yT_done[par], 1)

            def chunk(n, par):
                c = 2 * n + par
                lo = act_e.value_load(iter_at[0:1, bass.ds(c, 1)], min_val=1, max_val=NC_ * LIST)
                hi = act_e.value_load(iter_at[0:1, bass.ds(c + 1, 1)], min_val=1, max_val=NC_ * LIST)
                with act_e.Fori(lo, hi) as i:
                    at = nc.s_assert_within(act_e.snap(c * LIST + (i - lo) * QUAD), 0, NC_ * LIST - QUAD, skip_runtime_bounds_check_because="a chunk has at most LIST places")
                    for u in range(2):
                        act_e.wait_ge(weighted_done[u], i)
                        for k in range(2):
                            act_e.dma_start(comb_b[u][INTER * k:INTER * (k + 1), :],
                                            comb_dram[bass.ds(at + 2 * u + k, 1), :].broadcast_to([INTER, CT])
                                            ).then_inc(comb_in[u], 16)
                    for u in range(2):
                        act_e.wait_ge(gate_mm[u], i + 1)
                        act_e.wait_ge(weighted_done[u], i)
                        nc.scalar.activation(silu[u][:], gate_ps[u][:], ACT.Silu).then_inc(silu_done[u], 1)
                act_e.wait_ge(y_mm[par], n + 1)
                act_e.wait_ge(yT_mm[par], n + 1)
                for q in range(BPC):
                    w = slice(SEQ * q, SEQ * (q + 1))
                    ins = nc.scalar.activation(yT[par][:, w], out_ps[par][:, w], ACT.Identity,
                                               scale=modT[:, GB, bass.ds(c * BPC + q, 1)])
                ins.then_inc(yT_done[par], 1)

            with act_e.Fori(0, NC_ // 2) as n:
                chunk(n, 0)
                chunk(n, 1)

        @block.tensor
        def _(pe):
            pe.wait_ge(weights_in, 16 * 7)
            pe.wait_ge(consts_done, 6)
            nc.tensor.matmul(bank[0][:, 0:D], wqT_sb[:], wkT_sb[:], start=True, stop=True).then_inc(mod_mm, 1)
            pe.wait_ge(siluc_done, 1)
            for k in range(NMOD):
                nc.tensor.matmul(bank[1][:, k * BATCH:(k + 1) * BATCH], wmod_sb[:, k * D:(k + 1) * D],
                                 silu_c[:], start=True, stop=True)
            nc.tensor.matmul(bank[2][0:BATCH, 0:D], silu_c[:], wmod_sb[:, GA * D:(GA + 1) * D],
                             start=True, stop=True).then_inc(mod_mm, 1)
            pe.wait_ge(mod_ready, 1)
            for b in range(BATCH):
                ins = nc.tensor.matmul(bank[3 + b // 4][:, (b % 4) * D:(b % 4 + 1) * D],
                                       ident[0:BATCH, b:b + 1].broadcast_to([BATCH, P]), ga_row[:],
                                       start=True, stop=True)
                if b % 4 == 3:
                    ins.then_inc(gab_mm, 1)
            pe.wait_ge(gab_ready, BATCH // 4)
            pe.wait_ge(wqk_ready, 1)

            def transposes(k, dst, c):
                pe.wait_ge(xn_done[k], c + 1)
                for t in range(TPC):
                    ins = nc.tensor.transpose(dst[:, t * P:(t + 1) * P], xn[k][:, t, :], ident[:])
                ins.then_inc(xnT_done[k], 1)

            def attend_a(c):
                wait(pe, pT_done, BPC * c - 1)
                transposes(0, bank[0], c)

            def attend_b(c):
                wait(pe, pT_done, BPC * c)
                pe.wait_ge(hT_done, c + 1)
                nc.tensor.matmul(bank[1][:], wqk[:], hT[:], start=True, stop=True).then_inc(g_mm, 1)
                wait(pe, x2_done, c)
                for t in range(TPC):
                    ins = nc.tensor.matmul(bank[2][:, t * D:(t + 1) * D], hT[:, t * P:(t + 1) * P], wv_sb[:],
                                           start=True, stop=True)
                ins.then_inc(v_mm, 1)

            def attend_c(c):
                pe.wait_ge(gT_done, c + 1)
                for q in range(BPC):
                    wait(pe, probs_done, BPC * (c - 1) + q + 1)
                    r0 = slice(SEQ * q, SEQ * q + P)
                    r1 = slice(SEQ * q + P, SEQ * (q + 1))
                    s = bank[3 + q]
                    nc.tensor.matmul(s[:, 0:P], gT[:, r0], hT[:, r0], start=True, stop=False)
                    nc.tensor.matmul(s[:, 0:P], ident[:], causal[:], start=False, stop=True)
                    nc.tensor.matmul(s[:, P:2 * P], gT[:, r1], hT[:, r0], start=True, stop=True)
                    nc.tensor.matmul(s[:, 2 * P:SW], gT[:, r1], hT[:, r1], start=True, stop=False)
                    nc.tensor.matmul(s[:, 2 * P:SW], ident[:], causal[:], start=False,
                                     stop=True).then_inc(s_mm, 1)

            def attend_d(c):
                for q in range(BPC):
                    pe.wait_ge(probs_done, BPC * c + q + 1)
                    for r in range(3):
                        ins = nc.tensor.transpose(bank[q][:, r * P:(r + 1) * P], probs[:, q, r * P:(r + 1) * P],
                                                  ident[:])
                    ins.then_inc(pT_mm, 1)
                pe.wait_ge(v_done, c + 1)
                for q in range(BPC):
                    pe.wait_ge(pT_done, BPC * c + q + 1)
                    o = bank[2]
                    at = 2 * q * D
                    nc.tensor.matmul(o[:, at:at + D], probsT[:, q, 0:P], v_sb[:, 2 * q, :], start=True, stop=True)
                    nc.tensor.matmul(o[:, at + D:at + 2 * D], probsT[:, q, P:2 * P], v_sb[:, 2 * q, :],
                                     start=True, stop=False)
                    ins = nc.tensor.matmul(o[:, at + D:at + 2 * D], probsT[:, q, 2 * P:SW], v_sb[:, 2 * q + 1, :],
                                           start=False, stop=True)
                ins.then_inc(o_mm, 1)

            def route_a(c):
                wait(pe, h2T_done, c)
                transposes(1, bank[5], c)

            def route_b(c):
                pe.wait_ge(h2T_done, c + 1)
                wait(pe, logit_exp, c)
                for t in range(TPC):
                    at = c * CT + t * P
                    ins = nc.tensor.matmul(bank[6][:, t * E:(t + 1) * E], h2T[:, at:at + P], gate_sb[:],
                                           start=True, stop=True)
                ins.then_inc(logit_mm, 1)

            def route_c(c):
                pe.wait_ge(comb_done, c + 1)
                wait(pe, combT_done, c)
                for t in range(TPC):
                    ins = nc.tensor.transpose(bank[7][0:EA, t * P:(t + 1) * P], comb[:, t, :], ident[:])
                ins.then_inc(combT_mm, 1)

            for c in range(NC_ + 1):
                if c < NC_:
                    attend_a(c)
                if c >= 1:
                    route_a(c - 1)
                if c < NC_:
                    attend_b(c)
                if c >= 1:
                    route_b(c - 1)
                if c < NC_:
                    attend_c(c)
                    attend_d(c)
                if c >= 1:
                    route_c(c - 1)

            pe.wait_ge(act_done, 1)
            nc.tensor.matmul(bank[5][0:EA, 0:NC_], tri[:], act[:], start=True, stop=True)
            nc.tensor.matmul(bank[6][0:1, 0:NC_], ones[0:EA, :], act[:], start=True, stop=True).then_inc(pos_mm, 1)
            pe.wait_ge(onehot_done, 1)
            for c in range(NC_):
                nc.tensor.matmul(bank[3 + c // 4][0:1, (c % 4) * LIST:(c % 4 + 1) * LIST], expert_no[0:EA, :],
                                 onehot[:, c, :], start=True, stop=True).then_inc(list_mm, 1)
            for c in range(NC_):
                wait(pe, comb_list_done, c - 1)
                nc.tensor.matmul(bank[c % 2][0:LIST, :], onehot[:, c, :], combT[:, c, :],
                                 start=True, stop=True).then_inc(comb_list_mm, 1)
            pe.wait_ge(comb_list_done, NC_)
            pe.wait_ge(tables_done, 1)

            for u in range(2):
                for s in (gate_mm[u], up_mm[u], down_mm[u]):
                    pe.sem_inc(s, 1)
            for par in range(2):
                pe.sem_inc(yT_mm[par], 1)

            def gate_up(u, i, c):
                xs = h2T[:, bass.ds(c * CT, CT)]
                pe.wait_ge(gu_in[u], i * 32)
                pe.wait_ge(silu_done[u], i)
                nc.tensor.matmul(gate_ps[u][:], gu[u][:, 0, :], xs, start=True,
                                 stop=True).then_inc(gate_mm[u], 1)
                pe.wait_ge(hidden_done[u], i)
                nc.tensor.matmul(up_ps[u][:], gu[u][:, 1, :], xs, start=True,
                                 stop=True).then_inc(up_mm[u], 1)

            def down(u, i, par, last=False):
                pe.wait_ge(wd_in[u], i * 32)
                pe.wait_ge(hidden_done[u], i + 1)
                nc.tensor.matmul(out_ps[par][:], wd[u][:], act_h[u][:], start=False, stop=last,
                                 skip_group_check=True).then_inc(down_mm[u], 1)

            def transpose_out(n1, par):
                pe.wait_ge(yT_done[par], n1 + 1)
                pe.wait_ge(y_done[par], n1)
                for t in range(TPC):
                    ins = nc.tensor.transpose(t_ps[par][:, t * P:(t + 1) * P], yT[par][:, t * P:(t + 1) * P],
                                              ident[:])
                ins.then_inc(yT_mm[par], 1)

            def chunk(n, par, has_next=True, out_before=True):
                c = 2 * n + par
                lo = pe.value_load(iter_at[0:1, bass.ds(c, 1)], min_val=1, max_val=NC_ * LIST)
                last = pe.value_load(iter_last[0:1, bass.ds(c, 1)], min_val=2, max_val=NC_ * LIST)
                pe.wait_ge(yT_done[par], n + 1)
                nc.tensor.matmul(out_ps[par][:], zeros[:], h2T[:, 0:CT], start=True, stop=False,
                                 skip_group_check=True)
                with pe.Fori(lo, last) as i:
                    gate_up(1, i, c)
                    down(0, i, par)
                    gate_up(0, i + 1, c)
                    down(1, i, par)
                gate_up(1, last, c)
                down(0, last, par)
                if has_next:
                    gate_up(0, last + 1, c + 1)
                pe.wait_ge(wd_in[1], last * 32)
                pe.wait_ge(hidden_done[1], last + 1)
                nc.tensor.matmul(out_ps[par][:], wd[1][:], act_h[1][:], start=False, stop=True,
                                 skip_group_check=True).then_inc(down_mm[1], 1)
                pe.wait_ge(down_mm[1], last + 1)
                pe.sem_inc(y_mm[par], 1)
                if out_before:
                    transpose_out(n + par, 1 - par)

            gate_up(0, 1, 0)
            chunk(0, 0, out_before=False)
            chunk(0, 1)
            with pe.Fori(1, NC_ // 2 - 1) as n:
                chunk(n, 0)
                chunk(n, 1)
            chunk(NC_ // 2 - 1, 0)
            chunk(NC_ // 2 - 1, 1, has_next=False)
            transpose_out(NC_ // 2, 1)

        @block.vector
        def _(dve):
            v = nc.vector
            n = [0]

            def link(ins):
                n[0] += 1
                ins.then_inc(dve_step, 1)
                dve.wait_ge(dve_step, n[0])

            link(v.memset(ones[:], 1.0))
            v.memset(seg_e[:], 1.0)
            v.memset(seg_g[:], 1.0)
            v.memset(zeros[:], 0.0)
            v.memset(zero8[:], 0.0)
            link(v.memset(comb[:], 1.0))
            v.memset(seg_e[:, :, 0:1], 0.0)
            link(v.memset(seg_g[:, :, 0:1], 0.0))
            dve.wait_ge(expc_done, 1)
            link(v.tensor_scalar(silu_c[:], silu_c[:], 1.0, None, ALU.add))
            link(v.reciprocal(silu_c[:], silu_c[:]))
            v.tensor_tensor(silu_c[:], silu_c[:], cT_sb[:], ALU.mult).then_inc(siluc_done, 1)
            dve.wait_ge(mod_mm, 2)
            link(v.tensor_copy(modT[:].rearrange("p k b -> p (k b)"), bank[1][:, 0:NMOD * BATCH]))
            for k in (CA, CB):
                v.tensor_scalar(modT[:, k, :], modT[:, k, :], 1.0, None, ALU.add)
            link(v.tensor_copy(ga_row[:], bank[2][0:BATCH, 0:D]))
            for g, w in ((modT[:, GB, :], BATCH), (ga_row[:], D)):
                m = mod_tmp[0:g.shape[0], :, 0:w]
                link(v.tensor_scalar(m[:, 0, :], g, 0.0, None, ALU.is_ge))
                link(v.scalar_tensor_tensor(out=m[:, 0, :], in0=g, scalar=0.25, in1=m[:, 0, :],
                                            op0=ALU.max, op1=ALU.mult))
                link(v.tensor_scalar(m[:, 1, :], g, 0.0, None, ALU.is_lt))
                link(v.scalar_tensor_tensor(out=m[:, 1, :], in0=g, scalar=-0.25, in1=m[:, 1, :],
                                            op0=ALU.min, op1=ALU.mult))
                link(v.tensor_tensor(g, m[:, 0, :], m[:, 1, :], ALU.add))
            dve.sem_inc(mod_ready, 1)

            def moments(k, c):
                if k == 0:
                    dve.wait_ge(x_in[c], 16)
                for t in range(TPC):
                    ins = v.bn_stats(stats[k][:, t, :], x_all[:, TPC * c + t, :])
                link(ins)
                for t in range(TPC):
                    ins = v.bn_aggr(mv[k][:, t, :], stats[k][:, t, :])
                link(ins)
                v.tensor_scalar(veps[k][:], mv[k][:, :, 1], EPS, None, ALU.add).then_inc(var_done[k], 1)

            def normalise(k, c):
                dve.wait_ge(rstd_done[k], c + 1)
                wait(dve, xnT_done[k], c)
                for t in range(TPC):
                    ins = v.tensor_scalar(xn[k][:, t, :], x_all[:, TPC * c + t, :], mv[k][:, t, 0:1],
                                          rstd[k][:, t:t + 1], ALU.subtract, ALU.mult)
                ins.then_inc(xn_done[k], 1)

            def gated_values(c):
                dve.wait_ge(v_mm, c + 1)
                if c == 0:
                    dve.wait_ge(gab_ready, BATCH // 4)
                wait(dve, o_mm, c)
                for q in range(BPC):
                    ga = ga_all[:, BPC * c + q:BPC * c + q + 1, :].broadcast_to([P, 2, D])
                    ins = v.tensor_tensor(v_sb[:, 2 * q:2 * q + 2, :],
                                          bank[2][:, 2 * q * D:(2 * q + 2) * D].rearrange("p (t d) -> p t d", t=2),
                                          ga, ALU.mult)
                ins.then_inc(v_done, 1)

            def maxima(c):
                wait(dve, probs_done, BPC * c)
                for q in range(BPC):
                    dve.wait_ge(s_mm, BPC * c + q + 1)
                    for r, w in enumerate((slice(0, P), slice(P, SW))):
                        ins = v.tensor_reduce(neg_max[:, 2 * q + r:2 * q + r + 1], bank[3 + q][:, w], AX_X, ALU.max,
                                              negate=True)
                    ins.then_inc(max_done, 1)

            def residual(c):
                dve.wait_ge(probs_done, BPC * (c + 1))
                link(v.reciprocal(rsum[:], sums[:]))
                dve.wait_ge(o_mm, c + 1)
                for t in range(TPC):
                    ins = v.scalar_tensor_tensor(out=x_all[:, TPC * c + t, :], in0=bank[2][:, t * D:(t + 1) * D],
                                                 scalar=rsum[:, t:t + 1], in1=x_all[:, TPC * c + t, :],
                                                 op0=ALU.mult, op1=ALU.add)
                link(ins)
                dve.sem_inc(x2_done, 1)

            def pick(vals, seg, kth, sorted8, sorted_gt, gt, eq, run, k, n_in):
                b = [P, TPC, n_in]
                v.tensor_tensor(sorted_gt, sorted8, kth.broadcast_to([P, TPC, 8]), ALU.is_gt)
                v.tensor_tensor(gt, vals, kth.broadcast_to(b), ALU.is_gt)
                link(v.tensor_tensor(eq, vals, kth.broadcast_to(b), ALU.is_equal))
                v.tensor_reduce(cnt[:], sorted_gt, AX_X, ALU.add)
                link(v.tensor_tensor_scan(run.rearrange("p t e -> p (t e)"), seg.rearrange("p t e -> p (t e)"),
                                          eq.rearrange("p t e -> p (t e)"), 0.0, ALU.mult, ALU.add))
                link(v.tensor_tensor(run, run, cnt[:].unsqueeze(2).broadcast_to(b), ALU.add))
                link(v.scalar_tensor_tensor(out=run, in0=run, scalar=float(k), in1=eq, op0=ALU.is_le, op1=ALU.mult))
                link(v.tensor_tensor(gt, gt, run, ALU.add))

            def routing(c):
                dve.wait_ge(logit_exp, c + 1)
                link(v.tensor_scalar(score[:], score[:], 1.0, None, ALU.add))
                link(v.reciprocal(score[:], score[:]))
                link(v.tensor_tensor(score[:], score[:], bias_sb[:].unsqueeze(1).broadcast_to([P, TPC, E]), ALU.add))
                link(v.tensor_reduce(grp[:].rearrange("p t g -> p (t g)"),
                                     score[:].rearrange("p t (g e) -> p (t g) e", g=GROUPS), AX_X, ALU.max))
                for t in range(TPC):
                    ins = v.max(grp_top[:, t, :], grp[:, t, :])
                link(ins)
                pick(grp[:], seg_g[:], grp_top[:, :, TOPG - 1:TOPG], grp_top[:], top_gt[:], grp_gt[:], grp_eq[:],
                     grp_run[:], TOPG, GROUPS)
                link(v.tensor_tensor(masked[:].rearrange("p t (g e) -> p (t g) e", g=GROUPS),
                                     score[:].rearrange("p t (g e) -> p (t g) e", g=GROUPS),
                                     grp_gt[:].rearrange("p t g -> p (t g)").unsqueeze(2)
                                     .broadcast_to([P, TPC * GROUPS, GE]), ALU.mult))
                for t in range(TPC):
                    ins = v.max(top[:, t, :], masked[:, t, :])
                link(ins)
                pick(masked[:], seg_e[:], top[:, :, TOPK - 1:TOPK], top[:], top_gt[:], e_gt[:], e_eq[:],
                     e_run[:], TOPK, E)
                v.tensor_tensor(masked[:], masked[:], e_gt[:], ALU.mult)
                link(v.tensor_reduce(wsum[:], top[:, :, 0:TOPK], AX_X, ALU.add))
                link(v.tensor_scalar(wsum[:], wsum[:], 1e-8, None, ALU.add))
                link(v.reciprocal(wsum[:], wsum[:]))
                wait(dve, combT_mm, c)
                v.tensor_tensor(comb[:, :, NSH:EA], masked[:], wsum[:].unsqueeze(2).broadcast_to([P, TPC, E]),
                                ALU.mult).then_inc(comb_done, 1)

            def activity(c):
                dve.wait_ge(combT_done, c + 1)
                v.tensor_reduce(act_max[:, c:c + 1], combT[:, c, :], AX_X, ALU.max).then_inc(act_max_done, 1)

            for c in range(NC_ + 1):
                if c < NC_:
                    moments(0, c)
                if c >= 1:
                    moments(1, c - 1)
                if c < NC_:
                    normalise(0, c)
                if c >= 1:
                    normalise(1, c - 1)
                if c < NC_:
                    gated_values(c)
                    maxima(c)
                if c >= 1:
                    routing(c - 1)
                if c < NC_:
                    residual(c)
                if c >= 1:
                    activity(c - 1)

            dve.wait_ge(act_max_done, NC_)
            v.tensor_scalar(act[:], act_max[:], 0.0, None, ALU.is_gt).then_inc(act_done, 1)
            dve.wait_ge(pos_mm, 1)
            v.tensor_copy(n_iter[:], bank[6][0:1, 0:NC_])
            link(v.tensor_copy(pos[:], bank[5][0:EA, 0:NC_]))
            for c in range(NC_):
                ins = v.tensor_scalar(onehot[:, c, :], place_no[0:EA, :], pos[:, c:c + 1], act[:, c:c + 1],
                                      ALU.is_equal, ALU.mult)
            ins.then_inc(onehot_done, 1)
            nq = LIST // QUAD
            link(v.tensor_tensor(before[:], quad_start[:].unsqueeze(1).broadcast_to([1, NC_, nq]),
                                 n_iter[:].unsqueeze(2).broadcast_to([1, NC_, nq]), ALU.is_lt))
            link(v.tensor_reduce(n_iter[:], before[:], AX_X, ALU.add))
            link(v.tensor_scalar(n_iter[:], n_iter[:], 2.0, None, ALU.max))
            v.memset(iter_f[:, 0:1], 1.0)
            link(v.tensor_tensor_scan(iter_f[:, 1:NC_ + 1], n_iter[:], zero8[:], 1.0, ALU.add, ALU.add))
            v.tensor_copy(iter_at[:], iter_f[:])
            v.tensor_scalar(iter_last[:], iter_f[:, 1:NC_ + 1], -1.0, None, ALU.add)
            dve.wait_ge(list_mm, NC_)
            for h in range(2):
                ins = v.tensor_copy(lists[:, h * 4 * LIST:(h + 1) * 4 * LIST], bank[3 + h][0:1, 0:4 * LIST])
            link(ins)
            for u in range(2):
                dve.sem_inc(hidden_done[u], 1)
            for par in range(2):
                dve.sem_inc(y_done[par], 1)
            dve.sem_inc(tables_done, 1)

            def finish(n1, par, first=False):
                c = 2 * n1 + par - 2
                dve.wait_ge(yT_mm[par], n1 + 1)
                if not first:
                    dve.wait_ge(y_out[par], 16 * n1 - 16)
                v.tensor_tensor(y[par][:].rearrange("p t d -> p (t d)"), t_ps[par][:],
                                x_all[:, bass.ds(c * TPC, TPC), :].rearrange("p t d -> p (t d)"),
                                ALU.add).then_inc(y_done[par], 1)

            def chunk(n, par, before_it=True, first=False):
                c = 2 * n + par
                lo = dve.value_load(iter_at[0:1, bass.ds(c, 1)], min_val=1, max_val=NC_ * LIST)
                hi = dve.value_load(iter_at[0:1, bass.ds(c + 1, 1)], min_val=1, max_val=NC_ * LIST)
                with dve.Fori(lo, hi) as i:
                    for u in range(2):
                        dve.wait_ge(weighted_done[u], i + 1)
                        dve.wait_ge(up_mm[u], i + 1)
                        dve.wait_ge(down_mm[u], i)
                        v.tensor_tensor(act_h[u][:], up_ps[u][:], act_g[u][:], ALU.mult).then_inc(hidden_done[u], 1)
                if before_it:
                    finish(n + par, 1 - par, first)

            chunk(0, 0, before_it=False)
            chunk(0, 1, first=True)
            chunk(1, 0, first=True)
            chunk(1, 1)
            with dve.Fori(2, NC_ // 2) as m:
                chunk(m, 0)
                chunk(m, 1)
            finish(NC_ // 2, 1)


_OUT = "out"


def kernel(**inputs):
    import numpy as np
    import concourse.bacc as bacc
    from concourse.bass_utils import run_bass_kernel_spmd as run

    a = {k[3:]: np.asarray(v) for k, v in inputs.items()}
    sh = lambda w: w.reshape(NSH, INTER, D)
    gates = np.concatenate([sh(a["ffn_sg_w"]), a["ffn_eg_w"]])
    ups = np.concatenate([sh(a["ffn_su_w"]), a["ffn_eu_w"]])
    downs = np.concatenate([a["ffn_sd_w"].reshape(D, NSH, INTER).transpose(1, 0, 2), a["ffn_ed_w"]])
    arrays = {
        "x": a["attn_x"],
        "cT": a["c"].T,
        "wmod": a["wmod"],
        "wqT": a["attn_Wq"].T,
        "wkT": a["attn_Wk"].T,
        "wv": a["attn_Wv"],
        "gate_wT": a["ffn_gate_w"].T,
        "gate_bias": a["ffn_gate_bias"],
        "w_gu": np.concatenate([gates, ups], axis=1).transpose(0, 2, 1),
        "w_down": downs.transpose(0, 2, 1),
    }
    arrays = {k: np.ascontiguousarray(v) for k, v in arrays.items()}
    nc = bacc.Bacc("TRN2", target_bir_lowering=False, num_devices=1)
    args = [nc.dram_tensor(k, v.shape, mybir.dt.from_np(v.dtype), kind="ExternalInput").ap()
            for k, v in arrays.items()]
    args.append(nc.dram_tensor("comb_dram", [NC_ * LIST, CT], F32).ap())
    args.append(nc.dram_tensor(_OUT, (BATCH, SEQ, D), F32, kind="ExternalOutput").ap())
    build(nc, *args)
    r = run(nc, [arrays], core_ids=[0])
    return r.results[0][_OUT]
```

```python
from contextlib import ExitStack

import concourse.bass as bass
from concourse import mybir

F32 = mybir.dt.float32
F32R = mybir.dt.float32r
I32 = mybir.dt.int32
ALU = mybir.AluOpType
ACT = mybir.ActivationFunctionType
AX_X = mybir.AxisListType.X

P = 128
BATCH, SEQ, D = 16, 256, 128
TOKENS = BATCH * SEQ
CT = 512
NC_ = TOKENS // CT
TPC = CT // P
BPC = CT // SEQ
E, INTER, GROUPS, TOPG, TOPK = 64, 64, 8, 4, 6
GE = E // GROUPS
NSH = 2
EA = E + NSH
LIST = E + 2
MAX_LOOPS = (LIST - 2) // 4
NMOD = 6
SA, CA, GA, SB, CB, GB = range(NMOD)
SW = P + SEQ
EPS = 1e-5
BIG = 1e30


def build(nc, x, cT, wmod, wqT, wkT, wv, gate_wT, gate_bias, w_gu, w_down, comb_dram, out):
    with ExitStack() as ctx:
        def sb(name, shape, dt=F32):
            return ctx.enter_context(nc.sbuf_tensor(name, shape, dt))

        def sem(name):
            return ctx.enter_context(nc.semaphore(name))

        bank = [ctx.enter_context(nc.psum_tensor(f"bank{i}", [P, 512], F32)) for i in range(8)]

        ident = sb("ident", [P, P])
        causal = sb("causal", [P, P])
        tri = sb("tri", [E, E])
        place_no = sb("place_no", [P, LIST])
        expert_no = sb("expert_no", [P, 1])
        ones = sb("ones", [P, 1])
        loop_start = sb("loop_start", [1, MAX_LOOPS])
        zeros = sb("zeros", [P, TOKENS // P])
        seg_e = sb("seg_e", [P, TPC, E])
        seg_g = sb("seg_g", [P, TPC, GROUPS])
        half_neg = sb("half_neg", [P, TPC])
        cT_sb = sb("cT_sb", [P, BATCH])
        silu_c = sb("silu_c", [P, BATCH])
        mod_tmp = sb("mod_tmp", [P, 2, D])
        wmod_sb = sb("wmod_sb", [P, NMOD * D])
        wqT_sb = sb("wqT_sb", [P, D])
        wkT_sb = sb("wkT_sb", [P, D])
        wv_sb = sb("wv_sb", [P, D])
        wqk = sb("wqk", [P, D])
        gate_sb = sb("gate_sb", [P, E])
        bias_sb = sb("bias_sb", [P, E])
        modT = sb("modT", [P, NMOD, BATCH])
        ga_row = sb("ga_row", [BATCH, D])
        ga_all = sb("ga_all", [P, BATCH, D])

        x_all = sb("x_all", [P, TPC * NC_, D])
        stats = [sb(f"stats{n}", [P, TPC, 6]) for n in (1, 2)]
        mv = [sb(f"mean_var{n}", [P, TPC, 2]) for n in (1, 2)]
        veps = [sb(f"var_eps{n}", [P, TPC]) for n in (1, 2)]
        rstd = [sb(f"rstd{n}", [P, TPC]) for n in (1, 2)]
        xn = [sb(f"xn{n}", [P, TPC, D]) for n in (1, 2)]
        hT = sb("hT", [P, CT])
        gT = sb("gT", [P, CT])
        v_sb = sb("v_sb", [P, TPC, D])
        neg_max = sb("neg_max", [P, TPC])
        sums = sb("sums", [P, TPC])
        rsum = sb("rsum", [P, TPC])
        probs = sb("probs", [P, BPC, SW])
        probsT = sb("probsT", [P, BPC, SW])
        h2T = sb("h2T", [P, CT])
        h2_hi = sb("h2_hi", [P, TOKENS], F32R)
        h2_lo = sb("h2_lo", [P, TOKENS], F32R)
        score = sb("score", [P, TPC, E])
        grp = sb("grp", [P, TPC, GROUPS])
        grp_top = sb("grp_top", [P, TPC, 8])
        grp_gt = sb("grp_gt", [P, TPC, GROUPS])
        grp_eq = sb("grp_eq", [P, TPC, GROUPS])
        grp_run = sb("grp_run", [P, TPC, GROUPS])
        masked = sb("masked", [P, TPC, E])
        top = sb("top", [P, TPC, 8])
        top_gt = sb("top_gt", [P, TPC, 8])
        cnt = sb("cnt", [P, TPC])
        e_gt = sb("e_gt", [P, TPC, E])
        e_eq = sb("e_eq", [P, TPC, E])
        e_run = sb("e_run", [P, TPC, E])
        wsum = sb("wsum", [P, TPC])
        comb = sb("comb", [P, TPC, E])
        combT = sb("combT", [E, 2, CT])
        act_max = sb("act_max", [E, NC_])
        act_any = sb("act_any", [E, 1])
        act = sb("act", [E, 1])
        pos = sb("pos", [E, 1])
        onehot = sb("onehot", [E, LIST])
        lists = sb("lists", [1, LIST], I32)
        before = sb("before", [1, MAX_LOOPS])
        n_act = sb("n_act", [1, 1])
        n_loops = sb("n_loops", [1, 1])
        ends = sb("ends", [1, 2], I32)

        gu_raw = sb("gu_raw", [P, 2, 2 * INTER])
        gu_hi = [sb(f"gu_hi{u}", [P, 2, 2 * INTER], F32R) for u in range(2)]
        gu_lo = [sb(f"gu_lo{u}", [P, 2, 2 * INTER], F32R) for u in range(2)]
        wd = [sb(f"wd{u}", [P, D]) for u in range(2)]
        comb_b = [sb(f"comb_b{u}", [P, TOKENS]) for u in range(2)]
        silu = [sb(f"silu{n}", [P, CT]) for n in range(2)]
        weighted = [sb(f"weighted{n}", [P, CT]) for n in range(2)]
        hidden = [sb(f"hidden{n}", [P, CT]) for n in range(2)]
        acc = sb("acc", [P, TOKENS])
        yT = [sb(f"yT{n}", [P, CT]) for n in range(2)]
        y = [sb(f"y{n}", [P, TPC, D]) for n in range(2)]

        weights_in = sem("weights_in")
        x_in = [sem(f"x_in{c}") for c in range(NC_)]
        consts_done = sem("consts_done")
        pool_step = sem("pool_step")
        dve_step = sem("dve_step")
        act_step = sem("act_step")
        expc_done = sem("expc_done")
        siluc_done = sem("siluc_done")
        mod_mm = sem("mod_mm")
        mod_ready = sem("mod_ready")
        gab_mm = sem("gab_mm")
        gab_ready = sem("gab_ready")
        wqk_ready = sem("wqk_ready")
        var_done = [sem(f"var{n}_done") for n in (1, 2)]
        rstd_done = [sem(f"rstd{n}_done") for n in (1, 2)]
        xn_done = [sem(f"xn{n}_done") for n in (1, 2)]
        xnT_done = [sem(f"xnT{n}_done") for n in (1, 2)]
        hT_done = sem("hT_done")
        g_mm = sem("g_mm")
        gT_done = sem("gT_done")
        v_mm = sem("v_mm")
        v_done = sem("v_done")
        s_mm = sem("s_mm")
        max_done = sem("max_done")
        probs_done = sem("probs_done")
        pT_mm = sem("pT_mm")
        pT_done = sem("pT_done")
        o_mm = sem("o_mm")
        x2_done = sem("x2_done")
        h2T_done = sem("h2T_done")
        logit_mm = sem("logit_mm")
        logit_exp = sem("logit_exp")
        comb_done = sem("comb_done")
        combT_mm = sem("combT_mm")
        combT_done = sem("combT_done")
        act_max_done = sem("act_max_done")
        act_done = sem("act_done")
        pos_mm = sem("pos_mm")
        onehot_done = sem("onehot_done")
        list_mm = sem("list_mm")
        h2_split = sem("h2_split")
        comb_out = [sem(f"comb_out{n}") for n in range(2)]
        tables_done = sem("tables_done")

        gu_in = sem("gu_in")
        gu_high = sem("gu_high")
        gu_split = sem("gu_split")
        wd_in = [sem(f"wd_in{u}") for u in range(2)]
        comb_in = [[sem(f"comb_in{u}_{h}") for h in range(2)] for u in range(2)]
        gate_mm = sem("gate_mm")
        up_mm = sem("up_mm")
        silu_done = sem("silu_done")
        weighted_done = sem("weighted_done")
        hidden_done = sem("hidden_done")
        down_mm = sem("down_mm")
        acc_done = sem("acc_done")
        yT_done = sem("yT_done")
        yT_mm = sem("yT_mm")
        y_done = sem("y_done")
        y_out = [sem(f"y_out{n}") for n in range(2)]

        x_v = x.rearrange("b (s p) d -> p (b s) d", p=P)
        out_v = out.rearrange("b (s p) d -> p (b s) d", p=P)
        gate_ps = [bank[0], bank[2]]
        up_ps = [bank[1], bank[3]]
        out_ps = [bank[4], bank[5]]
        t_ps = [bank[6], bank[7]]

        def steps(at, c):
            return at + (NC_ + c + 1)

        def chunk_cols(c):
            return slice(CT * c, CT * (c + 1))

        def tiles(c):
            return slice(TPC * c, TPC * (c + 1))

        def wait(eng, s, n):
            if not isinstance(n, int) or n > 0:
                eng.wait_ge(s, n)

        block = ctx.enter_context(nc.Block())

        @block.sync
        def _(sp):
            for dst, src in ((cT_sb[:], cT), (wqT_sb[:], wqT), (wkT_sb[:], wkT), (wmod_sb[:], wmod),
                             (wv_sb[:], wv), (gate_sb[:], gate_wT),
                             (bias_sb[:], gate_bias.partition_broadcast(P))):
                sp.dma_start(dst, src).then_inc(weights_in, 16)
            for c in range(NC_):
                sp.dma_start(x_all[:, tiles(c), :], x_v[:, tiles(c), :]).then_inc(x_in[c], 16)
            for k in range(NSH):
                sp.dma_start(gu_raw[:, :, INTER * k:INTER * (k + 1)],
                             w_gu[E + k].rearrange("p (h n) -> p h n", h=2)).then_inc(gu_in, 16)
                sp.dma_start(wd[0][INTER * k:INTER * (k + 1), :], w_down[E + k]).then_inc(wd_in[0], 16)
            sp.wait_ge(consts_done, 7)
            sp.dma_start(comb_dram[E:E + 1, :].rearrange("o (p f) -> (o p) f", p=P), zeros[:]).then_inc(comb_out[0], 16)
            for c in range(NC_):
                sp.wait_ge(combT_done, c + 1)
                sp.dma_start(comb_dram[0:E, chunk_cols(c)], combT[:, c % 2, :]).then_inc(comb_out[c % 2], 16)
            sp.wait_ge(tables_done, 1)
            for n in range(2):
                sp.wait_ge(comb_out[n], 16 * (NC_ // 2 + 1 - n))

            def load_pass(q, u):
                who = [sp.value_load(lists[0:1, bass.ds(2 * q + k, 1)], min_val=0, max_val=E)
                       for k in range(2)]
                sp.wait_ge(gu_split, q * NC_ + NC_)
                for k in range(2):
                    sp.dma_start(gu_raw[:, :, INTER * k:INTER * (k + 1)],
                                 w_gu[bass.ds(who[k], 1)].rearrange("e p (h n) -> (e p) h n", h=2)
                                 ).then_inc(gu_in, 16)
                sp.wait_ge(down_mm, q * NC_ + 1)
                for h in range(2):
                    w = slice(TOKENS // 2 * h, TOKENS // 2 * (h + 1))
                    for k in range(2):
                        sp.dma_start(comb_b[u][INTER * k:INTER * (k + 1), w],
                                     comb_dram[bass.ds(who[k], 1), w].broadcast_to([INTER, TOKENS // 2])
                                     ).then_inc(comb_in[u][h], 16)
                    if h == 0:
                        for k in range(2):
                            sp.dma_start(wd[u][INTER * k:INTER * (k + 1), :],
                                         w_down[bass.ds(who[k], 1)].rearrange("e p n -> (e p) n")
                                         ).then_inc(wd_in[u], 16)

            last = sp.value_load(ends[0:1, 0:1], min_val=2, max_val=2 * MAX_LOOPS)
            with sp.Fori(0, last, 2) as q:
                load_pass(q, 1)
                load_pass(q + 1, 0)
            load_pass(last, 1)
            for c in range(NC_):
                sp.wait_ge(y_done, c + 1)
                sp.dma_start(out_v[:, tiles(c), :], y[c % 2][:]).then_inc(y_out[c % 2], 16)
            for n in range(2):
                sp.wait_ge(y_out[n], 16 * NC_ // 2)

        @block.gpsimd
        def _(pool):
            n = [0]

            def link(ins):
                n[0] += 1
                ins.then_inc(pool_step, 1)
                pool.wait_ge(pool_step, n[0])

            link(nc.gpsimd.memset(ident[:], 0.0))
            link(nc.gpsimd.memset(causal[:], 0.0))
            link(nc.gpsimd.memset(tri[:], 1.0))
            nc.gpsimd.affine_select(out=ident[:], in_=ident[:], compare_op=ALU.not_equal, fill=1.0,
                                    base=0, pattern=[[-1, P]], channel_multiplier=1).then_inc(consts_done, 1)
            nc.gpsimd.affine_select(out=causal[:], in_=causal[:], compare_op=ALU.is_ge, fill=-BIG,
                                    base=0, pattern=[[-1, P]], channel_multiplier=1).then_inc(consts_done, 1)
            nc.gpsimd.affine_select(out=tri[:], in_=tri[:], compare_op=ALU.is_gt, fill=0.0,
                                    base=0, pattern=[[1, E]], channel_multiplier=-1).then_inc(consts_done, 1)
            nc.gpsimd.iota(place_no[:], pattern=[[1, LIST]], base=0, channel_multiplier=0,
                           allow_small_or_imprecise_dtypes=True).then_inc(consts_done, 1)
            nc.gpsimd.iota(expert_no[:], pattern=[[0, 1]], base=-E, channel_multiplier=1,
                           allow_small_or_imprecise_dtypes=True).then_inc(consts_done, 1)
            nc.gpsimd.iota(loop_start[:], pattern=[[4, MAX_LOOPS]], base=2, channel_multiplier=0,
                           allow_small_or_imprecise_dtypes=True).then_inc(consts_done, 1)
            nc.gpsimd.memset(zeros[:], 0.0).then_inc(consts_done, 1)
            link(nc.gpsimd.memset(half_neg[:], -0.5))

            def deviation(k, c):
                pool.wait_ge(var_done[k], c + 1)
                nc.gpsimd.tensor_tensor(rstd[k][:], veps[k][:], half_neg[:], ALU.pow).then_inc(rstd_done[k], 1)

            def split_rows(c):
                pool.wait_ge(h2T_done, c + 1)
                link(nc.gpsimd.tensor_copy(h2_hi[:, chunk_cols(c)], h2T[:]))
                nc.gpsimd.tensor_tensor(h2_lo[:, chunk_cols(c)], h2T[:], h2_hi[:, chunk_cols(c)],
                                        ALU.subtract).then_inc(h2_split, 1)

            for c in range(NC_ + 1):
                if c < NC_:
                    deviation(0, c)
                if c >= 1:
                    deviation(1, c - 1)
                    split_rows(c - 1)

            def weight_pass(at, u):
                for c in range(NC_):
                    if c % (NC_ // 2) == 0:
                        pool.wait_ge(comb_in[u][c // (NC_ // 2)], at * 2 + (16 + 16 * u))
                    pool.wait_ge(silu_done, steps(at, c))
                    nc.gpsimd.tensor_tensor(weighted[c % 2][:], silu[c % 2][:], comb_b[u][:, chunk_cols(c)],
                                            ALU.mult).then_inc(weighted_done, 1)

            pool.wait_ge(tables_done, 1)
            last = pool.value_load(ends[0:1, 1:2], min_val=2 * NC_, max_val=2 * MAX_LOOPS * NC_)
            with pool.Fori(0, last, 2 * NC_) as at:
                weight_pass(at, 1)
                weight_pass(at + NC_, 0)
            weight_pass(last, 1)

        @block.scalar
        def _(act_e):
            act_e.wait_ge(weights_in, 16 * 7)
            nc.scalar.activation(silu_c[:], cT_sb[:], ACT.Exp, scale=-1.0).then_inc(expc_done, 1)
            act_e.wait_ge(mod_mm, 1)
            nc.scalar.activation(wqk[:], bank[0][:, 0:D], ACT.Copy, scale=float(D) ** -0.5).then_inc(wqk_ready, 1)
            for n in range(BATCH // 4):
                act_e.wait_ge(gab_mm, n + 1)
                nc.scalar.copy(ga_all[:, 4 * n:4 * n + 4, :].rearrange("p b d -> p (b d)"),
                               bank[3 + n][:]).then_inc(gab_ready, 1)

            def modulate(dst, k, src, shift, scale, c, done):
                for q in range(BPC):
                    b = BPC * c + q
                    w = slice(SEQ * q, SEQ * (q + 1))
                    ins = nc.scalar.activation(dst[:, w], src[:, w], ACT.Identity,
                                               bias=modT[:, shift, b:b + 1], scale=modT[:, scale, b:b + 1])
                ins.then_inc(done, 1)

            def attend_a(c):
                act_e.wait_ge(xnT_done[0], c + 1)
                wait(act_e, s_mm, BPC * c)
                if c == 0:
                    act_e.wait_ge(mod_ready, 1)
                modulate(hT, 0, bank[0], SA, CA, c, hT_done)
                act_e.wait_ge(g_mm, c + 1)
                nc.scalar.copy(gT[:], bank[1][:]).then_inc(gT_done, 1)

            def attend_b(c):
                for q in range(BPC):
                    act_e.wait_ge(max_done, BPC * c + q + 1)
                    wait(act_e, pT_mm, BPC * (c - 1) + q + 1)
                    wait(act_e, x2_done, c)
                    for r, w in enumerate((slice(0, P), slice(P, SW))):
                        ins = nc.scalar.activation(probs[:, q, w], bank[3 + q][:, w], ACT.Exp,
                                                   bias=neg_max[:, 2 * q + r:2 * q + r + 1],
                                                   accum_out=sums[:, 2 * q + r:2 * q + r + 1])
                    ins.then_inc(probs_done, 1)
                for q in range(BPC):
                    act_e.wait_ge(pT_mm, BPC * c + q + 1)
                    wait(act_e, o_mm, c)
                    nc.scalar.copy(probsT[:, q, :], bank[q][:, 0:SW]).then_inc(pT_done, 1)

            def route_a(c):
                act_e.wait_ge(xnT_done[1], c + 1)
                wait(act_e, logit_mm, c)
                wait(act_e, h2_split, c)
                modulate(h2T, 1, bank[5], SB, CB, c, h2T_done)

            def route_b(c):
                act_e.wait_ge(logit_mm, c + 1)
                wait(act_e, comb_done, c)
                nc.scalar.activation(score[:].rearrange("p t e -> p (t e)"), bank[6][:, 0:TPC * E], ACT.Exp,
                                     scale=-1.0).then_inc(logit_exp, 1)

            def route_c(c):
                act_e.wait_ge(combT_mm, c + 1)
                if c >= 2:
                    act_e.wait_ge(comb_out[c % 2], 16 * (c // 2 + 1 - c % 2))
                    act_e.wait_ge(act_max_done, c - 1)
                nc.scalar.copy(combT[:, c % 2, :], bank[7][0:E, :]).then_inc(combT_done, 1)

            def silu_step(at, c):
                act_e.wait_ge(gate_mm, steps(at, c))
                nc.scalar.activation(silu[c % 2][:], gate_ps[c % 2][:], ACT.Silu).then_inc(silu_done, 1)

            def gated_sums(at, c):
                act_e.wait_ge(acc_done, steps(at, c))
                wait(act_e, yT_mm, c - 1)
                for q in range(BPC):
                    w = slice(SEQ * q, SEQ * (q + 1))
                    ins = nc.scalar.activation(yT[c % 2][:, w], acc[:, CT * c + SEQ * q:CT * c + SEQ * (q + 1)],
                                               ACT.Identity, scale=modT[:, GB, BPC * c + q:BPC * c + q + 1])
                ins.then_inc(yT_done, 1)

            for c in range(NC_ + 1):
                if c < NC_:
                    attend_a(c)
                if c >= 1:
                    route_a(c - 1)
                    route_b(c - 1)
                if c == NC_:
                    silu_step(-NC_, 0)
                    silu_step(-NC_, 1)
                if c < NC_:
                    attend_b(c)
                if c >= 1:
                    route_c(c - 1)

            for c in range(2, NC_):
                silu_step(-NC_, c)
            act_e.wait_ge(tables_done, 1)
            last = act_e.value_load(ends[0:1, 1:2], min_val=2 * NC_, max_val=2 * MAX_LOOPS * NC_)
            with act_e.Fori(0, last, 2 * NC_) as at:
                for c in range(2 * NC_):
                    silu_step(at, c)
            for c in range(NC_ + 2):
                if c < NC_:
                    silu_step(last, c)
                if c >= 2:
                    gated_sums(last, c - 2)

        @block.tensor
        def _(pe):
            pe.wait_ge(weights_in, 16 * 7)
            pe.wait_ge(consts_done, 7)
            nc.tensor.matmul(bank[0][:, 0:D], wqT_sb[:], wkT_sb[:], start=True, stop=True).then_inc(mod_mm, 1)
            pe.wait_ge(siluc_done, 1)
            for k in range(NMOD):
                nc.tensor.matmul(bank[1][:, k * BATCH:(k + 1) * BATCH], wmod_sb[:, k * D:(k + 1) * D],
                                 silu_c[:], start=True, stop=True)
            nc.tensor.matmul(bank[2][0:BATCH, 0:D], silu_c[:], wmod_sb[:, GA * D:(GA + 1) * D],
                             start=True, stop=True).then_inc(mod_mm, 1)
            pe.wait_ge(mod_ready, 1)
            for b in range(BATCH):
                ins = nc.tensor.matmul(bank[3 + b // 4][:, (b % 4) * D:(b % 4 + 1) * D],
                                       ident[0:BATCH, b:b + 1].broadcast_to([BATCH, P]), ga_row[:],
                                       start=True, stop=True)
                if b % 4 == 3:
                    ins.then_inc(gab_mm, 1)
            pe.wait_ge(gab_ready, BATCH // 4)
            pe.wait_ge(wqk_ready, 1)

            def transposes(k, dst, c):
                pe.wait_ge(xn_done[k], c + 1)
                for t in range(TPC):
                    ins = nc.tensor.transpose(dst[:, t * P:(t + 1) * P], xn[k][:, t, :], ident[:])
                ins.then_inc(xnT_done[k], 1)

            def attend_a(c):
                wait(pe, pT_done, BPC * c - 1)
                transposes(0, bank[0], c)

            def attend_b(c):
                wait(pe, pT_done, BPC * c)
                pe.wait_ge(hT_done, c + 1)
                nc.tensor.matmul(bank[1][:], wqk[:], hT[:], start=True, stop=True).then_inc(g_mm, 1)
                wait(pe, x2_done, c)
                for t in range(TPC):
                    ins = nc.tensor.matmul(bank[2][:, t * D:(t + 1) * D], hT[:, t * P:(t + 1) * P], wv_sb[:],
                                           start=True, stop=True)
                ins.then_inc(v_mm, 1)

            def attend_c(c):
                pe.wait_ge(gT_done, c + 1)
                for q in range(BPC):
                    wait(pe, probs_done, BPC * (c - 1) + q + 1)
                    r0 = slice(SEQ * q, SEQ * q + P)
                    r1 = slice(SEQ * q + P, SEQ * (q + 1))
                    s = bank[3 + q]
                    nc.tensor.matmul(s[:, 0:P], gT[:, r0], hT[:, r0], start=True, stop=False)
                    nc.tensor.matmul(s[:, 0:P], ident[:], causal[:], start=False, stop=True)
                    nc.tensor.matmul(s[:, P:2 * P], gT[:, r1], hT[:, r0], start=True, stop=True)
                    nc.tensor.matmul(s[:, 2 * P:SW], gT[:, r1], hT[:, r1], start=True, stop=False)
                    nc.tensor.matmul(s[:, 2 * P:SW], ident[:], causal[:], start=False,
                                     stop=True).then_inc(s_mm, 1)

            def attend_d(c):
                for q in range(BPC):
                    pe.wait_ge(probs_done, BPC * c + q + 1)
                    for r in range(3):
                        ins = nc.tensor.transpose(bank[q][:, r * P:(r + 1) * P], probs[:, q, r * P:(r + 1) * P],
                                                  ident[:])
                    ins.then_inc(pT_mm, 1)
                pe.wait_ge(v_done, c + 1)
                for q in range(BPC):
                    pe.wait_ge(pT_done, BPC * c + q + 1)
                    o = bank[2]
                    at = 2 * q * D
                    nc.tensor.matmul(o[:, at:at + D], probsT[:, q, 0:P], v_sb[:, 2 * q, :], start=True, stop=True)
                    nc.tensor.matmul(o[:, at + D:at + 2 * D], probsT[:, q, P:2 * P], v_sb[:, 2 * q, :],
                                     start=True, stop=False)
                    ins = nc.tensor.matmul(o[:, at + D:at + 2 * D], probsT[:, q, 2 * P:SW], v_sb[:, 2 * q + 1, :],
                                           start=False, stop=True)
                ins.then_inc(o_mm, 1)

            def route_a(c):
                wait(pe, h2T_done, c)
                transposes(1, bank[5], c)

            def route_b(c):
                pe.wait_ge(h2T_done, c + 1)
                wait(pe, logit_exp, c)
                for t in range(TPC):
                    ins = nc.tensor.matmul(bank[6][:, t * E:(t + 1) * E], h2T[:, t * P:(t + 1) * P], gate_sb[:],
                                           start=True, stop=True)
                ins.then_inc(logit_mm, 1)

            def route_c(c):
                pe.wait_ge(comb_done, c + 1)
                wait(pe, combT_done, c)
                for t in range(TPC):
                    ins = nc.tensor.transpose(bank[7][0:E, t * P:(t + 1) * P], comb[:, t, :], ident[:])
                ins.then_inc(combT_mm, 1)

            def gate_up(at, u, c):
                if c == 0:
                    pe.wait_ge(gu_split, at + 2 * NC_)
                if isinstance(at, int):
                    pe.wait_ge(h2_split, c + 1)
                hi, lo = h2_hi[:, chunk_cols(c)], h2_lo[:, chunk_cols(c)]
                for half, dst, done in ((0, gate_ps[c % 2], gate_mm), (1, up_ps[c % 2], up_mm)):
                    nc.tensor.matmul(dst[:], gu_lo[u][:, half, :], hi, start=True, stop=False)
                    nc.tensor.matmul(dst[:], gu_hi[u][:, half, :], lo, start=False, stop=False)
                    nc.tensor.matmul(dst[:], gu_hi[u][:, half, :], hi, start=False, stop=True).then_inc(done, 1)

            def down(at, u, c):
                if c == 0:
                    pe.wait_ge(wd_in[u], at * 2 + (16 + 32 - 16 * u))
                if c < 0:
                    u = 1 - u
                wait(pe, acc_done, steps(at, c - 2))
                pe.wait_ge(hidden_done, steps(at, c))
                nc.tensor.matmul(out_ps[c % 2][:], wd[u][:], hidden[c % 2][:], start=True,
                                 stop=True).then_inc(down_mm, 1)

            def expert_pass(at, u):
                for c in range(NC_):
                    gate_up(at, u, c)
                    down(at, u, c - 1)

            def transpose_out(c):
                pe.wait_ge(yT_done, c + 1)
                wait(pe, y_done, c - 1)
                for t in range(TPC):
                    ins = nc.tensor.transpose(t_ps[c % 2][:, t * P:(t + 1) * P], yT[c % 2][:, t * P:(t + 1) * P],
                                              ident[:])
                ins.then_inc(yT_mm, 1)

            for c in range(NC_ + 1):
                if c < NC_:
                    attend_a(c)
                if c >= 1:
                    route_a(c - 1)
                if c < NC_:
                    attend_b(c)
                if c >= 1:
                    route_b(c - 1)
                if c < NC_:
                    attend_c(c)
                    attend_d(c)
                if c >= 1 and c < NC_:
                    route_c(c - 1)

            gate_up(-NC_, 0, 0)
            gate_up(-NC_, 0, 1)
            route_c(NC_ - 1)
            down(-NC_, 0, 0)
            gate_up(-NC_, 0, 2)
            pe.wait_ge(act_done, 1)
            nc.tensor.matmul(bank[6][0:E, 0:1], tri[:], act[:], start=True, stop=True)
            nc.tensor.matmul(bank[6][0:1, 2:3], ones[0:E, :], act[:], start=True, stop=True).then_inc(pos_mm, 1)
            down(-NC_, 0, 1)
            gate_up(-NC_, 0, 3)
            pe.wait_ge(onehot_done, 1)
            nc.tensor.matmul(bank[7][0:1, 0:LIST], expert_no[0:E, :], onehot[:], start=True,
                             stop=True).then_inc(list_mm, 1)
            down(-NC_, 0, 2)
            for c in range(4, NC_):
                gate_up(-NC_, 0, c)
                down(-NC_, 0, c - 1)
            pe.wait_ge(tables_done, 1)
            last = pe.value_load(ends[0:1, 1:2], min_val=2 * NC_, max_val=2 * MAX_LOOPS * NC_)
            with pe.Fori(0, last, 2 * NC_) as at:
                expert_pass(at, 1)
                expert_pass(at + NC_, 0)
            for c in range(NC_ + 3):
                if c < NC_:
                    gate_up(last, 1, c)
                if c >= 3:
                    transpose_out(c - 3)
                if c <= NC_:
                    down(last, 1, c - 1)

        @block.vector
        def _(dve):
            v = nc.vector
            n = [0]

            def link(ins):
                n[0] += 1
                ins.then_inc(dve_step, 1)
                dve.wait_ge(dve_step, n[0])

            link(v.memset(ones[:], 1.0))
            v.memset(seg_e[:], 1.0)
            link(v.memset(seg_g[:], 1.0))
            v.memset(seg_e[:, :, 0:1], 0.0)
            link(v.memset(seg_g[:, :, 0:1], 0.0))
            dve.wait_ge(expc_done, 1)
            link(v.tensor_scalar(silu_c[:], silu_c[:], 1.0, None, ALU.add))
            link(v.reciprocal(silu_c[:], silu_c[:]))
            v.tensor_tensor(silu_c[:], silu_c[:], cT_sb[:], ALU.mult).then_inc(siluc_done, 1)
            dve.wait_ge(mod_mm, 2)
            link(v.tensor_copy(modT[:].rearrange("p k b -> p (k b)"), bank[1][:, 0:NMOD * BATCH]))
            for k in (CA, CB):
                v.tensor_scalar(modT[:, k, :], modT[:, k, :], 1.0, None, ALU.add)
            link(v.tensor_copy(ga_row[:], bank[2][0:BATCH, 0:D]))
            for g, w in ((modT[:, GB, :], BATCH), (ga_row[:], D)):
                m = mod_tmp[0:g.shape[0], :, 0:w]
                link(v.tensor_scalar(m[:, 0, :], g, 0.0, None, ALU.is_ge))
                link(v.scalar_tensor_tensor(out=m[:, 0, :], in0=g, scalar=0.25, in1=m[:, 0, :],
                                            op0=ALU.max, op1=ALU.mult))
                link(v.tensor_scalar(m[:, 1, :], g, 0.0, None, ALU.is_lt))
                link(v.scalar_tensor_tensor(out=m[:, 1, :], in0=g, scalar=-0.25, in1=m[:, 1, :],
                                            op0=ALU.min, op1=ALU.mult))
                link(v.tensor_tensor(g, m[:, 0, :], m[:, 1, :], ALU.add))
            dve.sem_inc(mod_ready, 1)

            def moments(k, c):
                if k == 0:
                    dve.wait_ge(x_in[c], 16)
                for t in range(TPC):
                    ins = v.bn_stats(stats[k][:, t, :], x_all[:, TPC * c + t, :])
                link(ins)
                for t in range(TPC):
                    ins = v.bn_aggr(mv[k][:, t, :], stats[k][:, t, :])
                link(ins)
                v.tensor_scalar(veps[k][:], mv[k][:, :, 1], EPS, None, ALU.add).then_inc(var_done[k], 1)

            def normalise(k, c):
                dve.wait_ge(rstd_done[k], c + 1)
                wait(dve, xnT_done[k], c)
                for t in range(TPC):
                    ins = v.tensor_scalar(xn[k][:, t, :], x_all[:, TPC * c + t, :], mv[k][:, t, 0:1],
                                          rstd[k][:, t:t + 1], ALU.subtract, ALU.mult)
                ins.then_inc(xn_done[k], 1)

            def gated_values(c):
                dve.wait_ge(v_mm, c + 1)
                if c == 0:
                    dve.wait_ge(gab_ready, BATCH // 4)
                wait(dve, o_mm, c)
                for q in range(BPC):
                    ga = ga_all[:, BPC * c + q:BPC * c + q + 1, :].broadcast_to([P, 2, D])
                    ins = v.tensor_tensor(v_sb[:, 2 * q:2 * q + 2, :],
                                          bank[2][:, 2 * q * D:(2 * q + 2) * D].rearrange("p (t d) -> p t d", t=2),
                                          ga, ALU.mult)
                ins.then_inc(v_done, 1)

            def maxima(c):
                wait(dve, probs_done, BPC * c)
                for q in range(BPC):
                    dve.wait_ge(s_mm, BPC * c + q + 1)
                    for r, w in enumerate((slice(0, P), slice(P, SW))):
                        ins = v.tensor_reduce(neg_max[:, 2 * q + r:2 * q + r + 1], bank[3 + q][:, w], AX_X, ALU.max,
                                              negate=True)
                    ins.then_inc(max_done, 1)

            def residual(c):
                dve.wait_ge(probs_done, BPC * (c + 1))
                link(v.reciprocal(rsum[:], sums[:]))
                dve.wait_ge(o_mm, c + 1)
                for t in range(TPC):
                    ins = v.scalar_tensor_tensor(out=x_all[:, TPC * c + t, :], in0=bank[2][:, t * D:(t + 1) * D],
                                                 scalar=rsum[:, t:t + 1], in1=x_all[:, TPC * c + t, :],
                                                 op0=ALU.mult, op1=ALU.add)
                link(ins)
                dve.sem_inc(x2_done, 1)

            def pick(vals, seg, kth, sorted8, sorted_gt, gt, eq, run, k, n_in):
                b = [P, TPC, n_in]
                v.tensor_tensor(sorted_gt, sorted8, kth.broadcast_to([P, TPC, 8]), ALU.is_gt)
                v.tensor_tensor(gt, vals, kth.broadcast_to(b), ALU.is_gt)
                link(v.tensor_tensor(eq, vals, kth.broadcast_to(b), ALU.is_equal))
                v.tensor_reduce(cnt[:], sorted_gt, AX_X, ALU.add)
                link(v.tensor_tensor_scan(run.rearrange("p t e -> p (t e)"), seg.rearrange("p t e -> p (t e)"),
                                          eq.rearrange("p t e -> p (t e)"), 0.0, ALU.mult, ALU.add))
                link(v.tensor_tensor(run, run, cnt[:].unsqueeze(2).broadcast_to(b), ALU.add))
                link(v.scalar_tensor_tensor(out=run, in0=run, scalar=float(k), in1=eq, op0=ALU.is_le, op1=ALU.mult))
                link(v.tensor_tensor(gt, gt, run, ALU.add))

            def routing(c):
                dve.wait_ge(logit_exp, c + 1)
                link(v.tensor_scalar(score[:], score[:], 1.0, None, ALU.add))
                link(v.reciprocal(score[:], score[:]))
                link(v.tensor_tensor(score[:], score[:], bias_sb[:].unsqueeze(1).broadcast_to([P, TPC, E]), ALU.add))
                link(v.tensor_reduce(grp[:].rearrange("p t g -> p (t g)"),
                                     score[:].rearrange("p t (g e) -> p (t g) e", g=GROUPS), AX_X, ALU.max))
                for t in range(TPC):
                    ins = v.max(grp_top[:, t, :], grp[:, t, :])
                link(ins)
                pick(grp[:], seg_g[:], grp_top[:, :, TOPG - 1:TOPG], grp_top[:], top_gt[:], grp_gt[:], grp_eq[:],
                     grp_run[:], TOPG, GROUPS)
                link(v.tensor_tensor(masked[:].rearrange("p t (g e) -> p (t g) e", g=GROUPS),
                                     score[:].rearrange("p t (g e) -> p (t g) e", g=GROUPS),
                                     grp_gt[:].rearrange("p t g -> p (t g)").unsqueeze(2)
                                     .broadcast_to([P, TPC * GROUPS, GE]), ALU.mult))
                for t in range(TPC):
                    ins = v.max(top[:, t, :], masked[:, t, :])
                link(ins)
                pick(masked[:], seg_e[:], top[:, :, TOPK - 1:TOPK], top[:], top_gt[:], e_gt[:], e_eq[:],
                     e_run[:], TOPK, E)
                v.tensor_tensor(masked[:], masked[:], e_gt[:], ALU.mult)
                link(v.tensor_reduce(wsum[:], top[:, :, 0:TOPK], AX_X, ALU.add))
                link(v.tensor_scalar(wsum[:], wsum[:], 1e-8, None, ALU.add))
                link(v.reciprocal(wsum[:], wsum[:]))
                wait(dve, combT_mm, c)
                v.tensor_tensor(comb[:], masked[:], wsum[:].unsqueeze(2).broadcast_to([P, TPC, E]),
                                ALU.mult).then_inc(comb_done, 1)

            def activity(c):
                dve.wait_ge(combT_done, c + 1)
                v.tensor_reduce(act_max[:, c:c + 1], combT[:, c % 2, :], AX_X, ALU.max).then_inc(act_max_done, 1)

            def split_weights(at, u):
                dve.wait_ge(gu_in, at * 4 + 96)
                v.tensor_copy(gu_hi[u][:], gu_raw[:]).then_inc(gu_high, NC_)
                dve.wait_ge(gu_high, at + 3 * NC_)
                v.tensor_tensor(gu_lo[u][:], gu_raw[:], gu_hi[u][:], ALU.subtract).then_inc(gu_split, NC_)

            def hidden_step(at, c):
                if isinstance(at, int):
                    dve.wait_ge(silu_done, steps(at, c))
                    src = silu
                else:
                    dve.wait_ge(weighted_done, at + (c + 1))
                    src = weighted
                dve.wait_ge(up_mm, steps(at, c))
                v.tensor_tensor(hidden[c % 2][:], up_ps[c % 2][:], src[c % 2][:], ALU.mult).then_inc(hidden_done, 1)

            def sum_step(at, c):
                dve.wait_ge(down_mm, steps(at, c))
                a = acc[:, chunk_cols(c % NC_)]
                if isinstance(at, int):
                    v.tensor_copy(a, out_ps[c % 2][:]).then_inc(acc_done, 1)
                else:
                    v.tensor_tensor(a, out_ps[c % 2][:], a, ALU.add).then_inc(acc_done, 1)

            def sums_pass(at, u):
                for c in range(NC_):
                    hidden_step(at, c)
                    sum_step(at, c - 1)
                    if c == NC_ // 2:
                        split_weights(at, 1 - u)

            def finish(c):
                dve.wait_ge(yT_mm, c + 1)
                wait(dve, y_out[c % 2], 16 * (c // 2))
                v.tensor_tensor(y[c % 2][:].rearrange("p t d -> p (t d)"), t_ps[c % 2][:],
                                x_all[:, tiles(c), :].rearrange("p t d -> p (t d)"), ALU.add).then_inc(y_done, 1)

            v.memset(acc[:, chunk_cols(NC_ - 1)], 0.0)
            split_weights(-2 * NC_, 0)

            for c in range(NC_ + 1):
                if c < NC_:
                    moments(0, c)
                if c >= 1:
                    moments(1, c - 1)
                if c < NC_:
                    normalise(0, c)
                if c >= 1:
                    normalise(1, c - 1)
                if c < NC_:
                    gated_values(c)
                    maxima(c)
                if c >= 1:
                    routing(c - 1)
                if c < NC_:
                    residual(c)
                if c >= 1 and c < NC_:
                    activity(c - 1)

            hidden_step(-NC_, 0)
            hidden_step(-NC_, 1)
            activity(NC_ - 1)
            dve.wait_ge(act_max_done, NC_)
            link(v.tensor_reduce(act_any[:], act_max[:], AX_X, ALU.max))
            v.tensor_scalar(act[:], act_any[:], 0.0, None, ALU.is_gt).then_inc(act_done, 1)
            sum_step(-NC_, 0)
            hidden_step(-NC_, 2)
            dve.wait_ge(pos_mm, 1)
            v.tensor_copy(n_act[:], bank[6][0:1, 2:3])
            link(v.tensor_copy(pos[:], bank[6][0:E, 0:1]))
            v.tensor_scalar(onehot[:], place_no[0:E, :], pos[:], act[:], ALU.is_equal,
                            ALU.mult).then_inc(onehot_done, 1)
            link(v.tensor_scalar(before[:], loop_start[:], n_act[:], None, ALU.is_lt))
            link(v.tensor_reduce(n_loops[:], before[:], AX_X, ALU.add))
            link(v.tensor_scalar(n_loops[:], n_loops[:], 1.0, None, ALU.max))
            v.tensor_scalar(ends[:, 0:1], n_loops[:], 2.0, None, ALU.mult)
            v.tensor_scalar(ends[:, 1:2], n_loops[:], 2.0 * NC_, None, ALU.mult)
            sum_step(-NC_, 1)
            hidden_step(-NC_, 3)
            dve.wait_ge(list_mm, 1)
            link(v.tensor_scalar(lists[:], bank[7][0:1, 0:LIST], float(E), None, ALU.add))
            dve.sem_inc(tables_done, 1)
            sum_step(-NC_, 2)
            for c in range(4, NC_):
                hidden_step(-NC_, c)
                sum_step(-NC_, c - 1)
            split_weights(-NC_, 1)

            last = dve.value_load(ends[0:1, 1:2], min_val=2 * NC_, max_val=2 * MAX_LOOPS * NC_)
            with dve.Fori(0, last, 2 * NC_) as at:
                sums_pass(at, 1)
                sums_pass(at + NC_, 0)
            for c in range(NC_ + 3):
                if c < NC_:
                    hidden_step(last, c)
                if c <= NC_:
                    sum_step(last, c - 1)
                if c >= 3:
                    finish(c - 3)


_OUT = "out"


def kernel(**inputs):
    import numpy as np
    import concourse.bacc as bacc
    from concourse.bass_utils import run_bass_kernel_spmd as run

    a = {k[3:]: np.asarray(v) for k, v in inputs.items()}
    sh = lambda w: w.reshape(NSH, INTER, D)
    gates = np.concatenate([a["ffn_eg_w"], sh(a["ffn_sg_w"])])
    ups = np.concatenate([a["ffn_eu_w"], sh(a["ffn_su_w"])])
    downs = np.concatenate([a["ffn_ed_w"], a["ffn_sd_w"].reshape(D, NSH, INTER).transpose(1, 0, 2)])
    arrays = {
        "x": a["attn_x"],
        "cT": a["c"].T,
        "wmod": a["wmod"],
        "wqT": a["attn_Wq"].T,
        "wkT": a["attn_Wk"].T,
        "wv": a["attn_Wv"],
        "gate_wT": a["ffn_gate_w"].T,
        "gate_bias": a["ffn_gate_bias"],
        "w_gu": np.concatenate([gates, ups], axis=1).transpose(0, 2, 1),
        "w_down": downs.transpose(0, 2, 1),
    }
    arrays = {k: np.ascontiguousarray(v) for k, v in arrays.items()}
    nc = bacc.Bacc("TRN2", target_bir_lowering=False, num_devices=1)
    args = [nc.dram_tensor(k, v.shape, mybir.dt.from_np(v.dtype), kind="ExternalInput").ap()
            for k, v in arrays.items()]
    args.append(nc.dram_tensor("comb_dram", [E + 1, TOKENS], F32).ap())
    args.append(nc.dram_tensor(_OUT, (BATCH, SEQ, D), F32, kind="ExternalOutput").ap())
    build(nc, *args)
    r = run(nc, [arrays], core_ids=[0])
    return r.results[0][_OUT]
```

```python
from contextlib import ExitStack

import concourse.bass as bass
from concourse import mybir

F32 = mybir.dt.float32
F32R = mybir.dt.float32r
I32 = mybir.dt.int32
ALU = mybir.AluOpType
ACT = mybir.ActivationFunctionType
AX_X = mybir.AxisListType.X

P = 128
BATCH, SEQ, D = 16, 256, 128
TOKENS = BATCH * SEQ
CT = 512
NC_ = TOKENS // CT
TPC = CT // P
BPC = CT // SEQ
E, INTER, GROUPS, TOPG, TOPK = 64, 64, 8, 4, 6
GE = E // GROUPS
NSH = 2
ROUTE_STEPS = 11
LIST = E + 2
MAX_LOOPS = (LIST - 2) // 4
COMB_BEFORE = {1: NC_ - 2, 4: NC_ - 1}
FIRST_AT, FULL_AT = 1, 5
SPLIT_AT = 3
FP32_STEPS = NC_ - 2
NMOD = 6
SA, CA, GA, SB, CB, GB = range(NMOD)
SW = P + SEQ
EPS = 1e-5
BIG = 1e30


def build(nc, x, cT, wmod, wqT, wkT, wv, gate_wT, gate_bias, w_gu, w_down, ga_dram, comb_dram, out):
    with ExitStack() as ctx:
        def sb(name, shape, dt=F32):
            return ctx.enter_context(nc.sbuf_tensor(name, shape, dt))

        def sem(name):
            return ctx.enter_context(nc.semaphore(name))

        bank = [ctx.enter_context(nc.psum_tensor(f"bank{i}", [P, 512], F32)) for i in range(8)]

        ident = sb("ident", [P, P])
        causal = sb("causal", [P, P])
        tri = sb("tri", [E, E])
        place_no = sb("place_no", [P, LIST])
        expert_no = sb("expert_no", [P, 1])
        ones = sb("ones", [P, 1])
        loop_start = sb("loop_start", [1, MAX_LOOPS])
        zeros = sb("zeros", [P, TOKENS // P])
        half_neg = sb("half_neg", [P, TPC])
        cT_sb = sb("cT_sb", [P, BATCH])
        silu_c = sb("silu_c", [P, BATCH])
        mod_tmp = sb("mod_tmp", [P, 2, D])
        wmod_sb = sb("wmod_sb", [P, NMOD * D])
        wqT_sb = sb("wqT_sb", [P, D])
        wkT_sb = sb("wkT_sb", [P, D])
        wv_sb = sb("wv_sb", [P, D])
        wqk = sb("wqk", [P, D])
        gate_sb = sb("gate_sb", [P, E])
        bias_sb = sb("bias_sb", [P, E])
        modT = sb("modT", [P, NMOD, BATCH])
        ga_row = sb("ga_row", [BATCH, D])
        ga_all = sb("ga_all", [P, BATCH, D])

        x_all = sb("x_all", [P, TPC * NC_, D])
        stats = [sb(f"stats{n}", [P, TPC, 6]) for n in (1, 2)]
        mv = [sb(f"mean_var{n}", [P, TPC, 2]) for n in (1, 2)]
        veps = [sb(f"var_eps{n}", [P, TPC]) for n in (1, 2)]
        rstd = [sb(f"rstd{n}", [P, TPC]) for n in (1, 2)]
        xn = [sb(f"xn{n}", [P, TPC, D]) for n in (1, 2)]
        hT = [sb(f"hT{n}", [P, CT]) for n in range(2)]
        gT = [sb(f"gT{n}", [P, CT]) for n in range(2)]
        v_sb = [sb(f"v_sb{n}", [P, TPC, D]) for n in range(2)]
        neg_max = sb("neg_max", [P, TPC])
        sums = sb("sums", [P, TPC])
        rsum = sb("rsum", [P, TPC])
        shift = [sb(f"shift{n}", [P, TPC]) for n in (1, 2)]
        wv_g = [sb(f"wv_g{n}", [P, BPC, D]) for n in range(2)]
        probs = sb("probs", [P, BPC, SW])
        probsT = sb("probsT", [P, BPC, SW])
        h2T = sb("h2T", [P, CT])
        h2_hi = sb("h2_hi", [P, TOKENS], F32R)
        h2_lo = sb("h2_lo", [P, TOKENS], F32R)
        score = [sb(f"score{n}", [P, TPC, E]) for n in range(2)]
        grp = sb("grp", [P, TPC, GROUPS + 8 - TOPG])
        grp_top = sb("grp_top", [P, TPC, 8])
        grp_rest = sb("grp_rest", [P, TPC, GROUPS + 8 - TOPG])
        masked = sb("masked", [P, TPC, E + 8 - TOPK])
        top = sb("top", [P, TPC, 8])
        rest = sb("rest", [P, TPC, E + 8 - TOPK])
        wsum = sb("wsum", [P, TPC])
        comb = sb("comb", [P, TPC, E])
        combT = sb("combT", [E, 2, CT])
        comb_sum = sb("comb_sum", [E, NC_])
        act_any = sb("act_any", [E, 2])
        new = sb("new", [E, 1])
        base = sb("base", [E, 1])
        onehot_new = sb("onehot_new", [E, LIST])
        first_pair = sb("first_pair", [1, 2], I32)
        ones_sq = sb("ones_sq", [E, E])
        act = sb("act", [E, 2])
        pos = sb("pos", [E, 2])
        onehot = sb("onehot", [E, LIST])
        lists = sb("lists", [1, LIST], I32)
        before = sb("before", [1, MAX_LOOPS])
        n_act = sb("n_act", [1, 1])
        n_loops = sb("n_loops", [1, 1])
        ends = sb("ends", [1, 2], I32)

        gu_raw = sb("gu_raw", [P, 2, 2 * INTER])
        gu_hi = [sb(f"gu_hi{u}", [P, 2, 2 * INTER], F32R) for u in range(2)]
        gu_lo = [sb(f"gu_lo{u}", [P, 2, 2 * INTER], F32R) for u in range(2)]
        wd_raw = sb("wd_raw", [P, D])
        wd_shared = sb("wd_shared", [P, D])
        wd_hi = [sb(f"wd_hi{u}", [P, D], F32R) for u in range(2)]
        wd_lo = [sb(f"wd_lo{u}", [P, D], F32R) for u in range(2)]
        comb_b = [sb(f"comb_b{u}", [P, TOKENS]) for u in range(2)]
        silu = [sb(f"silu{n}", [P, CT]) for n in range(2)]
        weighted = [sb(f"weighted{n}", [P, CT]) for n in range(2)]
        hidden = [sb(f"hidden{n}", [P, CT]) for n in range(2)]
        hid_hi = [sb(f"hid_hi{n}", [P, CT], F32R) for n in range(2)]
        hid_lo = [sb(f"hid_lo{n}", [P, CT], F32R) for n in range(2)]
        acc = sb("acc", [P, TOKENS])
        yT = [sb(f"yT{n}", [P, CT]) for n in range(2)]
        y = [sb(f"y{n}", [P, TPC, D]) for n in range(2)]
        up_sb = [sb(f"up_sb{n}", [P, CT]) for n in range(2)]

        c_in = sem("c_in")
        wmod_in = sem("wmod_in")
        qk_in = sem("qk_in")
        weights_in = sem("weights_in")
        qk_mm = sem("qk_mm")
        ga_row_done = sem("ga_row_done")
        ga_out = sem("ga_out")
        ga_in = sem("ga_in")
        wvg_done = sem("wvg_done")
        stats_done = [sem(f"stats{n}_done") for n in (1, 2)]
        mean_done = [sem(f"mean{n}_done") for n in (1, 2)]
        rsum_done = sem("rsum_done")
        route_step = sem("route_step")
        up_copied = sem("up_copied")
        x_in = [sem(f"x_in{c}") for c in range(NC_)]
        consts_done = sem("consts_done")
        pool_step = sem("pool_step")
        dve_step = sem("dve_step")
        expc_done = sem("expc_done")
        siluc_done = sem("siluc_done")
        mod_mm = sem("mod_mm")
        mod_ready = sem("mod_ready")
        mod_copied = sem("mod_copied")
        wqk_ready = sem("wqk_ready")
        var_done = [sem(f"var{n}_done") for n in (1, 2)]
        rstd_done = [sem(f"rstd{n}_done") for n in (1, 2)]
        shift_done = [sem(f"shift{n}_done") for n in (1, 2)]
        xn_done = [sem(f"xn{n}_done") for n in (1, 2)]
        xnT_done = [sem(f"xnT{n}_done") for n in (1, 2)]
        hT_done = sem("hT_done")
        g_mm = sem("g_mm")
        gT_done = sem("gT_done")
        v_mm = sem("v_mm")
        v_done = sem("v_done")
        s_mm = sem("s_mm")
        max_done = sem("max_done")
        probs_done = sem("probs_done")
        pT_mm = sem("pT_mm")
        pT_done = sem("pT_done")
        o_mm = sem("o_mm")
        x2_done = sem("x2_done")
        h2T_done = sem("h2T_done")
        logit_mm = sem("logit_mm")
        logit_exp = sem("logit_exp")
        picked = sem("picked")
        chosen_done = sem("chosen_done")
        comb_done = sem("comb_done")
        combT_mm = sem("combT_mm")
        combT_done = sem("combT_done")
        act_any_done = sem("act_any_done")
        act_done = sem("act_done")
        pos_mm = sem("pos_mm")
        onehot_done = sem("onehot_done")
        list_mm = sem("list_mm")
        h2_high = sem("h2_high")
        h2_split = sem("h2_split")
        comb_out = [sem(f"comb_out{n}") for n in range(2)]
        pair_known = sem("pair_known")
        tables_done = sem("tables_done")

        shared_in = sem("shared_in")
        pair_in = sem("pair_in")
        pair_high = sem("pair_high")
        pair_split = sem("pair_split")
        comb_in = [[sem(f"comb_in{u}_{h}") for h in range(2)] for u in range(2)]
        gate_mm = sem("gate_mm")
        up_mm = sem("up_mm")
        silu_done = sem("silu_done")
        weighted_done = sem("weighted_done")
        hidden_done = sem("hidden_done")
        high_done = sem("high_done")
        low_done = sem("low_done")
        down_mm = sem("down_mm")
        acc_done = sem("acc_done")
        yT_done = sem("yT_done")
        yT_mm = sem("yT_mm")
        y_done = sem("y_done")
        y_out = [sem(f"y_out{n}") for n in range(2)]

        x_v = x.rearrange("b (s p) d -> p (b s) d", p=P)
        out_v = out.rearrange("b (s p) d -> p (b s) d", p=P)
        xnT_ps = [bank[0], bank[5]]
        g_ps, v_ps = bank[1], bank[2]
        attn_ps = [bank[3], bank[4]]
        combT_ps, logit_ps, o_ps = bank[5], bank[6], bank[7]
        gate_ps = [bank[0], bank[2]]
        up_ps = [bank[1], bank[3]]
        out_ps = [bank[4], bank[7]]
        t_ps = [bank[5], bank[6]]
        place_ps1, count_ps1, list_ps1 = bank[6][0:E, 0:1], bank[6][0:E, 2:3], bank[6][0:1, 4:6]
        place_ps2, count_ps2, list_ps2 = bank[6][0:E, 80:81], bank[6][0:1, 82:83], bank[6][0:1, 84:84 + LIST]

        def steps(at, c):
            return at + (NC_ + c + 1)

        def split_steps(at, c):
            return at + (NC_ + c + 1 - FP32_STEPS)

        def chunk_cols(c):
            return slice(CT * c, CT * (c + 1))

        def tiles(c):
            return slice(TPC * c, TPC * (c + 1))

        def wait(eng, s, n):
            if not isinstance(n, int) or n > 0:
                eng.wait_ge(s, n)

        block = ctx.enter_context(nc.Block())

        @block.sync
        def _(sp):
            def load_x(c):
                sp.dma_start(x_all[:, tiles(c), :], x_v[:, tiles(c), :]).then_inc(x_in[c], 16)

            sp.dma_start(cT_sb[:], cT).then_inc(c_in, 16)
            load_x(0)
            sp.dma_start(wmod_sb[:], wmod).then_inc(wmod_in, 16)
            for dst, src in ((wqT_sb[:], wqT), (wkT_sb[:], wkT)):
                sp.dma_start(dst, src).then_inc(qk_in, 16)
            for dst, src in ((wv_sb[:], wv), (gate_sb[:], gate_wT), (bias_sb[:], gate_bias.partition_broadcast(P))):
                sp.dma_start(dst, src).then_inc(weights_in, 16)
            for c in range(1, NC_):
                load_x(c)
            for k in range(NSH):
                sp.dma_start(gu_raw[:, :, INTER * k:INTER * (k + 1)],
                             w_gu[E + k].rearrange("p (h n) -> p h n", h=2)).then_inc(shared_in, 16)
                sp.dma_start(wd_shared[INTER * k:INTER * (k + 1), :], w_down[E + k]).then_inc(shared_in, 16)
            sp.wait_ge(ga_row_done, 1)
            sp.dma_start(ga_dram, ga_row[:]).then_inc(ga_out, 16)
            sp.wait_ge(ga_out, 16)
            sp.dma_start(ga_all[:].rearrange("p b d -> p (b d)"),
                         ga_dram.rearrange("b d -> (b d)").partition_broadcast(P)).then_inc(ga_in, 16)
            sp.wait_ge(consts_done, 8)
            sp.dma_start(comb_dram[E:E + 1, :].rearrange("o (p f) -> (o p) f", p=P), zeros[:]).then_inc(comb_out[0], 16)

            def store_comb(c):
                sp.wait_ge(combT_done, c + 1)
                sp.dma_start(comb_dram[0:E, chunk_cols(c)], combT[:, c % 2, :]).then_inc(comb_out[c % 2], 16)

            for c in range(NC_ - 1):
                store_comb(c)

            def experts_of(places):
                return [sp.value_load(places[k], min_val=0, max_val=E) for k in range(2)]

            def load_weights(who):
                for k in range(2):
                    sp.dma_start(gu_raw[:, :, INTER * k:INTER * (k + 1)],
                                 w_gu[bass.ds(who[k], 1)].rearrange("e p (h n) -> (e p) h n", h=2)
                                 ).then_inc(pair_in, 16)
                for k in range(2):
                    sp.dma_start(wd_raw[INTER * k:INTER * (k + 1), :],
                                 w_down[bass.ds(who[k], 1)].rearrange("e p n -> (e p) n")).then_inc(pair_in, 16)

            def load_comb(who, u, h):
                w = slice(TOKENS // 2 * h, TOKENS // 2 * (h + 1))
                for k in range(2):
                    sp.dma_start(comb_b[u][INTER * k:INTER * (k + 1), w],
                                 comb_dram[bass.ds(who[k], 1), w].broadcast_to([INTER, TOKENS // 2])
                                 ).then_inc(comb_in[u][h], 16)

            def load_pass(q, u):
                who = experts_of([lists[0:1, bass.ds(2 * q + k, 1)] for k in range(2)])
                sp.wait_ge(pair_split, q * NC_ + NC_)
                load_weights(who)
                if not isinstance(q, int):
                    sp.wait_ge(down_mm, q * NC_ + 1)
                for h in range(2):
                    load_comb(who, u, h)

            sp.wait_ge(pair_known, 1)
            who = experts_of([first_pair[0:1, k:k + 1] for k in range(2)])
            sp.wait_ge(pair_split, NC_)
            load_weights(who)
            sp.wait_ge(comb_out[0], 16 * (1 + NC_ // 4))
            sp.wait_ge(comb_out[1], 16 * (NC_ // 4))
            load_comb(who, 1, 0)
            store_comb(NC_ - 1)
            for n in range(2):
                sp.wait_ge(comb_out[n], 16 * (NC_ // 2 + 1 - n))
            load_comb(who, 1, 1)
            sp.wait_ge(tables_done, 1)
            load_pass(1, 0)
            last = sp.value_load(ends[0:1, 0:1], min_val=4, max_val=2 * MAX_LOOPS)
            with sp.Fori(2, last, 2) as q:
                load_pass(q, 1)
                load_pass(q + 1, 0)
            load_pass(last, 1)
            for c in range(NC_):
                sp.wait_ge(y_done, c + 1)
                sp.dma_start(out_v[:, tiles(c), :], y[c % 2][:]).then_inc(y_out[c % 2], 16)
            for n in range(2):
                sp.wait_ge(y_out[n], 16 * NC_ // 2)

        @block.gpsimd
        def _(pool):
            n = [0]

            def link(ins):
                n[0] += 1
                ins.then_inc(pool_step, 1)
                pool.wait_ge(pool_step, n[0])

            link(nc.gpsimd.memset(ident[:], 0.0))
            link(nc.gpsimd.memset(causal[:], 0.0))
            link(nc.gpsimd.memset(tri[:], 1.0))
            nc.gpsimd.memset(ones_sq[:], 1.0).then_inc(consts_done, 1)
            nc.gpsimd.affine_select(out=ident[:], in_=ident[:], compare_op=ALU.not_equal, fill=1.0,
                                    base=0, pattern=[[-1, P]], channel_multiplier=1).then_inc(consts_done, 1)
            nc.gpsimd.affine_select(out=causal[:], in_=causal[:], compare_op=ALU.is_ge, fill=-BIG,
                                    base=0, pattern=[[-1, P]], channel_multiplier=1).then_inc(consts_done, 1)
            nc.gpsimd.affine_select(out=tri[:], in_=tri[:], compare_op=ALU.is_gt, fill=0.0,
                                    base=0, pattern=[[1, E]], channel_multiplier=-1).then_inc(consts_done, 1)
            nc.gpsimd.iota(place_no[:], pattern=[[1, LIST]], base=0, channel_multiplier=0,
                           allow_small_or_imprecise_dtypes=True).then_inc(consts_done, 1)
            nc.gpsimd.iota(expert_no[:], pattern=[[0, 1]], base=-E, channel_multiplier=1,
                           allow_small_or_imprecise_dtypes=True).then_inc(consts_done, 1)
            nc.gpsimd.iota(loop_start[:], pattern=[[4, MAX_LOOPS]], base=2, channel_multiplier=0,
                           allow_small_or_imprecise_dtypes=True).then_inc(consts_done, 1)
            nc.gpsimd.memset(zeros[:], 0.0).then_inc(consts_done, 1)
            link(nc.gpsimd.memset(half_neg[:], -0.5))

            def deviation(k, c):
                pool.wait_ge(var_done[k], c + 1)
                nc.gpsimd.tensor_tensor(rstd[k][:], veps[k][:], half_neg[:], ALU.pow).then_inc(rstd_done[k], 1)

            def split_rows(c):
                pool.wait_ge(h2T_done, c + 1)
                nc.gpsimd.tensor_copy(h2_hi[:, chunk_cols(c)], h2T[:]).then_inc(h2_high, 1)
                pool.wait_ge(h2_high, c + 1)
                nc.gpsimd.tensor_tensor(h2_lo[:, chunk_cols(c)], h2T[:], h2_hi[:, chunk_cols(c)],
                                        ALU.subtract).then_inc(h2_split, 1)

            def gate_values(c):
                if c == 0:
                    pool.wait_ge(weights_in, 16 * 3)
                    pool.wait_ge(ga_in, 16)
                wait(pool, v_mm, c - 1)
                nc.gpsimd.tensor_tensor(wv_g[c % 2][:], wv_sb[:].unsqueeze(1).broadcast_to([P, BPC, D]),
                                        ga_all[:, BPC * c:BPC * (c + 1), :], ALU.mult).then_inc(wvg_done, 1)

            def shared_hidden(c):
                pool.wait_ge(up_copied, c + 1)
                nc.gpsimd.tensor_tensor(hidden[c % 2][:], silu[c % 2][:], up_sb[c % 2][:],
                                        ALU.mult).then_inc(hidden_done, 1)

            def combine(c):
                pool.wait_ge(picked, c + 1)
                wait(pool, combT_mm, c)
                nc.gpsimd.tensor_tensor(comb[:], masked[:, :, 0:E], rest[:, :, 0:E],
                                        ALU.subtract).then_inc(chosen_done, 1)
                pool.wait_ge(chosen_done, c + 1)
                nc.gpsimd.tensor_tensor(comb[:], comb[:], wsum[:].unsqueeze(2).broadcast_to([P, TPC, E]),
                                        ALU.mult).then_inc(comb_done, 1)

            deviation(0, 0)
            for i in range(NC_ + 2):
                if i + 1 < NC_:
                    deviation(0, i + 1)
                if i >= 4:
                    combine(i - 4)
                if 1 <= i <= NC_:
                    deviation(1, i - 1)
                if i < NC_:
                    gate_values(i)
                if i >= 2:
                    split_rows(i - 2)
            combine(NC_ - 2)
            for c in range(NC_):
                shared_hidden(c)

            def weight_pass(at, u, has_next=True):
                for c in range(NC_):
                    if c % (NC_ // 2) == 0:
                        pool.wait_ge(comb_in[u][c // (NC_ // 2)], at * 2 + (16 + 16 * u))
                    pool.wait_ge(silu_done, steps(at, c))
                    nc.gpsimd.tensor_tensor(weighted[c % 2][:], silu[c % 2][:], comb_b[u][:, chunk_cols(c)],
                                            ALU.mult).then_inc(weighted_done, 1)
                    n = 1 - u
                    if has_next and c == SPLIT_AT:
                        pool.wait_ge(pair_high, at + 3 * NC_)
                        nc.gpsimd.tensor_tensor(gu_lo[n][:, 0, :], gu_raw[:, 0, :], gu_hi[n][:, 0, :], ALU.subtract)
                    if has_next and c == SPLIT_AT + 1:
                        nc.gpsimd.tensor_tensor(gu_lo[n][:, 1, :], gu_raw[:, 1, :], gu_hi[n][:, 1, :], ALU.subtract)
                    if has_next and c == SPLIT_AT + 2:
                        nc.gpsimd.tensor_tensor(wd_lo[n][:], wd_raw[:], wd_hi[n][:],
                                                ALU.subtract).then_inc(pair_split, NC_)

            weight_pass(0, 1)
            weight_pass(NC_, 0)
            pool.wait_ge(tables_done, 1)
            last = pool.value_load(ends[0:1, 1:2], min_val=4 * NC_, max_val=2 * MAX_LOOPS * NC_)
            with pool.Fori(2 * NC_, last, 2 * NC_) as at:
                weight_pass(at, 1)
                weight_pass(at + NC_, 0)
            weight_pass(last, 1, has_next=False)

        @block.scalar
        def _(act_e):
            def modulate(dst, src, shift, scale, c):
                for q in range(BPC):
                    b = BPC * c + q
                    w = slice(SEQ * q, SEQ * (q + 1))
                    ins = nc.scalar.activation(dst[:, w], src[:, w], ACT.Identity,
                                               bias=modT[:, shift, b:b + 1], scale=modT[:, scale, b:b + 1])
                return ins

            def normalised(k, c):
                act_e.wait_ge(shift_done[k], c + 1)
                wait(act_e, xnT_done[k], c)
                for t in range(TPC):
                    ins = nc.scalar.activation(xn[k][:, t, :], x_all[:, TPC * c + t, :], ACT.Identity,
                                               bias=shift[k][:, t:t + 1], scale=rstd[k][:, t:t + 1])
                ins.then_inc(xn_done[k], 1)

            def modulated_rows(c):
                act_e.wait_ge(xnT_done[0], c + 1)
                wait(act_e, v_mm, c - 1)
                if c == 0:
                    act_e.wait_ge(mod_ready, 1)
                modulate(hT[c % 2], xnT_ps[0], SA, CA, c).then_inc(hT_done, 1)

            def key_side(c):
                act_e.wait_ge(g_mm, c + 1)
                nc.scalar.copy(gT[c % 2][:], g_ps[:]).then_inc(gT_done, 1)

            def values(c):
                act_e.wait_ge(v_mm, c + 1)
                wait(act_e, o_mm, c - 1)
                nc.scalar.copy(v_sb[c % 2][:].rearrange("p t d -> p (t d)"), v_ps[:]).then_inc(v_done, 1)

            def probabilities(c):
                for q in range(BPC):
                    act_e.wait_ge(max_done, BPC * c + q + 1)
                    wait(act_e, pT_mm, BPC * (c - 1) + q + 1)
                    wait(act_e, x2_done, c)
                    for r, w in enumerate((slice(0, P), slice(P, SW))):
                        ins = nc.scalar.activation(probs[:, q, w], attn_ps[q][:, w], ACT.Exp,
                                                   bias=neg_max[:, 2 * q + r:2 * q + r + 1],
                                                   accum_out=sums[:, 2 * q + r:2 * q + r + 1])
                    ins.then_inc(probs_done, 1)

            def transposed_probabilities(c):
                for q in range(BPC):
                    act_e.wait_ge(pT_mm, BPC * c + q + 1)
                    wait(act_e, o_mm, c)
                    nc.scalar.copy(probsT[:, q, :], attn_ps[q][:, 0:SW]).then_inc(pT_done, 1)

            def expert_rows(c):
                act_e.wait_ge(xnT_done[1], c + 1)
                wait(act_e, logit_mm, c)
                wait(act_e, h2_split, c)
                modulate(h2T, xnT_ps[1], SB, CB, c).then_inc(h2T_done, 1)

            def router_exp(c):
                act_e.wait_ge(logit_mm, c + 1)
                wait(act_e, picked, c - 1)
                nc.scalar.activation(score[c % 2][:].rearrange("p t e -> p (t e)"), logit_ps[:, 0:TPC * E], ACT.Exp,
                                     scale=-1.0).then_inc(logit_exp, 1)

            def comb_rows(c):
                act_e.wait_ge(combT_mm, c + 1)
                if c >= 2:
                    act_e.wait_ge(comb_out[c % 2], 16 * (c // 2 + 1 - c % 2))
                nc.scalar.activation(combT[:, c % 2, :], combT_ps[0:E, :], ACT.Copy,
                                     accum_out=comb_sum[:, c:c + 1]).then_inc(combT_done, 1)

            def silu_step(at, c):
                act_e.wait_ge(gate_mm, steps(at, c))
                nc.scalar.activation(silu[c % 2][:], gate_ps[c % 2][:], ACT.Silu).then_inc(silu_done, 1)

            def shared_step(c):
                silu_step(-NC_, c)
                act_e.wait_ge(up_mm, c + 1)
                nc.scalar.copy(up_sb[c % 2][:], up_ps[c % 2][:]).then_inc(up_copied, 1)
                if 0 < c <= FP32_STEPS:
                    act_e.wait_ge(down_mm, c)
                    nc.scalar.copy(acc[:, chunk_cols(c - 1)], out_ps[(c - 1) % 2][:]).then_inc(acc_done, 1)

            def high_step(at, c):
                act_e.wait_ge(hidden_done, steps(at, c))
                wait(act_e, down_mm, steps(at, c - 2))
                nc.scalar.copy(hid_hi[c % 2][:], hidden[c % 2][:]).then_inc(high_done, 1)

            def activation_pass(at, u):
                for c in range(NC_):
                    silu_step(at, c)
                    high_step(at, c - 1)
                    if c == SPLIT_AT:
                        act_e.wait_ge(pair_in, at * 8 + 2 * 64)
                        nc.scalar.copy(gu_hi[1 - u][:], gu_raw[:])
                        nc.scalar.copy(wd_hi[1 - u][:], wd_raw[:]).then_inc(pair_high, NC_)

            def gated_sums(at, c):
                act_e.wait_ge(acc_done, steps(at, c))
                wait(act_e, yT_mm, c - 1)
                for q in range(BPC):
                    w = slice(SEQ * q, SEQ * (q + 1))
                    ins = nc.scalar.activation(yT[c % 2][:, w], acc[:, CT * c + SEQ * q:CT * c + SEQ * (q + 1)],
                                               ACT.Identity, scale=modT[:, GB, BPC * c + q:BPC * c + q + 1])
                ins.then_inc(yT_done, 1)

            act_e.wait_ge(c_in, 16)
            nc.scalar.activation(silu_c[:], cT_sb[:], ACT.Exp, scale=-1.0).then_inc(expc_done, 1)
            normalised(0, 0)
            act_e.wait_ge(qk_mm, 1)
            nc.scalar.activation(wqk[:], bank[3][:, 0:D], ACT.Copy, scale=float(D) ** -0.5).then_inc(wqk_ready, 1)
            for i in range(NC_ + 2):
                if i < NC_:
                    modulated_rows(i)
                if 1 <= i <= NC_:
                    probabilities(i - 1)
                    values(i - 1)
                    transposed_probabilities(i - 1)
                if i < NC_:
                    key_side(i)
                if i >= 2:
                    normalised(1, i - 2)
                if i >= 2:
                    expert_rows(i - 2)
                if i + 1 < NC_:
                    normalised(0, i + 1)
                if i >= 2:
                    router_exp(i - 2)
                if i >= 4:
                    comb_rows(i - 4)
            for c in range(NC_):
                if c in COMB_BEFORE:
                    comb_rows(COMB_BEFORE[c])
                shared_step(c)
            high_step(-NC_, FP32_STEPS)
            activation_pass(0, 1)
            activation_pass(NC_, 0)
            act_e.wait_ge(tables_done, 1)
            last = act_e.value_load(ends[0:1, 1:2], min_val=4 * NC_, max_val=2 * MAX_LOOPS * NC_)
            with act_e.Fori(2 * NC_, last, 2 * NC_) as at:
                activation_pass(at, 1)
                activation_pass(at + NC_, 0)
            for c in range(NC_ + 2):
                if c < NC_:
                    silu_step(last, c)
                if c == 0:
                    high_step(last, -1)
                if c >= 2:
                    gated_sums(last, c - 2)

        @block.tensor
        def _(pe):
            pe.wait_ge(wmod_in, 16)
            pe.wait_ge(siluc_done, 1)
            for k in range(NMOD):
                ins = nc.tensor.matmul(bank[1][:, k * BATCH:(k + 1) * BATCH], wmod_sb[:, k * D:(k + 1) * D],
                                       silu_c[:], start=True, stop=True)
            ins.then_inc(mod_mm, 1)
            nc.tensor.matmul(bank[2][0:BATCH, 0:D], silu_c[:], wmod_sb[:, GA * D:(GA + 1) * D],
                             start=True, stop=True).then_inc(mod_mm, 1)
            pe.wait_ge(qk_in, 32)
            nc.tensor.matmul(bank[3][:, 0:D], wqT_sb[:], wkT_sb[:], start=True, stop=True).then_inc(qk_mm, 1)
            pe.wait_ge(consts_done, 8)

            def transposes(k, c):
                pe.wait_ge(xn_done[k], c + 1)
                for t in range(TPC):
                    ins = nc.tensor.transpose(xnT_ps[k][:, t * P:(t + 1) * P], xn[k][:, t, :], ident[:])
                ins.then_inc(xnT_done[k], 1)

            def first_rows(c):
                wait(pe, hT_done, c)
                transposes(0, c)

            def key_side(c):
                if c == 0:
                    pe.wait_ge(wqk_ready, 1)
                    pe.wait_ge(mod_copied, 2)
                pe.wait_ge(hT_done, c + 1)
                wait(pe, gT_done, c)
                nc.tensor.matmul(g_ps[:], wqk[:], hT[c % 2][:], start=True, stop=True).then_inc(g_mm, 1)

            def values(c):
                wait(pe, v_done, c)
                pe.wait_ge(wvg_done, c + 1)
                for t in range(TPC):
                    ins = nc.tensor.matmul(v_ps[:, t * D:(t + 1) * D], hT[c % 2][:, t * P:(t + 1) * P],
                                           wv_g[c % 2][:, t // 2, :], start=True, stop=True)
                ins.then_inc(v_mm, 1)

            def scores(c):
                pe.wait_ge(gT_done, c + 1)
                g, h = gT[c % 2], hT[c % 2]
                for q in range(BPC):
                    wait(pe, pT_done, BPC * (c - 1) + q + 1)
                    r0 = slice(SEQ * q, SEQ * q + P)
                    r1 = slice(SEQ * q + P, SEQ * (q + 1))
                    s = attn_ps[q]
                    nc.tensor.matmul(s[:, 0:P], g[:, r0], h[:, r0], start=True, stop=False)
                    nc.tensor.matmul(s[:, 0:P], ident[:], causal[:], start=False, stop=True)
                    nc.tensor.matmul(s[:, P:2 * P], g[:, r1], h[:, r0], start=True, stop=True)
                    nc.tensor.matmul(s[:, 2 * P:SW], g[:, r1], h[:, r1], start=True, stop=False)
                    nc.tensor.matmul(s[:, 2 * P:SW], ident[:], causal[:], start=False,
                                     stop=True).then_inc(s_mm, 1)

            def transposed_probabilities(c):
                for q in range(BPC):
                    pe.wait_ge(probs_done, BPC * c + q + 1)
                    for r in range(3):
                        ins = nc.tensor.transpose(attn_ps[q][:, r * P:(r + 1) * P], probs[:, q, r * P:(r + 1) * P],
                                                  ident[:])
                    ins.then_inc(pT_mm, 1)

            def attention_out(c):
                pe.wait_ge(v_done, c + 1)
                wait(pe, x2_done, c)
                v = v_sb[c % 2]
                for q in range(BPC):
                    pe.wait_ge(pT_done, BPC * c + q + 1)
                    at = 2 * q * D
                    nc.tensor.matmul(o_ps[:, at:at + D], probsT[:, q, 0:P], v[:, 2 * q, :], start=True, stop=True)
                    nc.tensor.matmul(o_ps[:, at + D:at + 2 * D], probsT[:, q, P:2 * P], v[:, 2 * q, :],
                                     start=True, stop=False)
                    ins = nc.tensor.matmul(o_ps[:, at + D:at + 2 * D], probsT[:, q, 2 * P:SW], v[:, 2 * q + 1, :],
                                           start=False, stop=True)
                ins.then_inc(o_mm, 1)

            def second_rows(c):
                wait(pe, combT_done, c - 2)
                wait(pe, h2T_done, c)
                transposes(1, c)

            def router(c):
                pe.wait_ge(h2T_done, c + 1)
                wait(pe, logit_exp, c)
                for t in range(TPC):
                    ins = nc.tensor.matmul(logit_ps[:, t * E:(t + 1) * E], h2T[:, t * P:(t + 1) * P], gate_sb[:],
                                           start=True, stop=True)
                ins.then_inc(logit_mm, 1)

            def comb_rows(c):
                pe.wait_ge(comb_done, c + 1)
                pe.wait_ge(h2T_done, min(c + 3, NC_))
                wait(pe, combT_done, c)
                for t in range(TPC):
                    ins = nc.tensor.transpose(combT_ps[0:E, t * P:(t + 1) * P], comb[:, t, :], ident[:])
                ins.then_inc(combT_mm, 1)

            def gate_up(at, u, c):
                if c == 0:
                    pe.wait_ge(pair_split, at + 2 * NC_)
                if isinstance(at, int):
                    pe.wait_ge(h2_split, c + 1)
                wait(pe, hidden_done, steps(at, c - 2))
                hi, lo = h2_hi[:, chunk_cols(c)], h2_lo[:, chunk_cols(c)]
                for half, dst, done in ((0, gate_ps[c % 2], gate_mm), (1, up_ps[c % 2], up_mm)):
                    nc.tensor.matmul(dst[:], gu_lo[u][:, half, :], hi, start=True, stop=False)
                    nc.tensor.matmul(dst[:], gu_hi[u][:, half, :], lo, start=False, stop=False)
                    nc.tensor.matmul(dst[:], gu_hi[u][:, half, :], hi, start=False, stop=True).then_inc(done, 1)

            def down(at, u, c):
                if c < 0:
                    u = 1 - u
                dst, hi, lo = out_ps[c % 2], hid_hi[c % 2], hid_lo[c % 2]
                pe.wait_ge(acc_done, steps(at, c - 2))
                pe.wait_ge(high_done, split_steps(at, c))
                nc.tensor.matmul(dst[:], wd_lo[u][:], hi[:], start=True, stop=False)
                nc.tensor.matmul(dst[:], wd_hi[u][:], hi[:], start=False, stop=False)
                pe.wait_ge(low_done, split_steps(at, c))
                nc.tensor.matmul(dst[:], wd_hi[u][:], lo[:], start=False, stop=True).then_inc(down_mm, 1)

            def float32_down(at, wd, c):
                wait(pe, acc_done, steps(at, c - 2))
                pe.wait_ge(hidden_done, steps(at, c))
                nc.tensor.matmul(out_ps[c % 2][:], wd[:], hidden[c % 2][:], start=True,
                                 stop=True).then_inc(down_mm, 1)

            def expert_pass(at, u):
                for c in range(NC_):
                    gate_up(at, u, c)
                    down(at, u, c - 2)

            def transpose_out(c):
                pe.wait_ge(yT_done, c + 1)
                wait(pe, y_done, c - 1)
                for t in range(TPC):
                    ins = nc.tensor.transpose(t_ps[c % 2][:, t * P:(t + 1) * P], yT[c % 2][:, t * P:(t + 1) * P],
                                              ident[:])
                ins.then_inc(yT_mm, 1)

            for i in range(NC_ + 2):
                if i < NC_:
                    first_rows(i)
                if 1 <= i <= NC_:
                    values(i - 1)
                if i < NC_:
                    key_side(i)
                if 1 <= i <= NC_:
                    transposed_probabilities(i - 1)
                    attention_out(i - 1)
                if i >= 2:
                    second_rows(i - 2)
                if i < NC_:
                    scores(i)
                if i >= 2:
                    router(i - 2)
                if i >= 4:
                    comb_rows(i - 4)

            for c in range(NC_):
                if c in COMB_BEFORE:
                    comb_rows(COMB_BEFORE[c])
                gate_up(-NC_, 0, c)
                if c == FIRST_AT:
                    pe.wait_ge(act_done, 1)
                    nc.tensor.matmul(place_ps1, tri[:], act[:, 0:1], start=True, stop=True)
                    nc.tensor.matmul(count_ps1, ones_sq[:], act[:, 0:1], start=True,
                                     stop=True).then_inc(pos_mm, 1)
                if c == FULL_AT:
                    pe.wait_ge(act_done, 2)
                    nc.tensor.matmul(place_ps2, tri[:], new[:], start=True, stop=True)
                    nc.tensor.matmul(count_ps2, ones[0:E, :], new[:], start=True,
                                     stop=True).then_inc(pos_mm, 1)
                if 0 < c <= FP32_STEPS:
                    float32_down(-NC_, wd_shared, c - 1)
                if c == FIRST_AT + 1:
                    pe.wait_ge(onehot_done, 1)
                    nc.tensor.matmul(list_ps1, expert_no[0:E, :], onehot[:, 0:2], start=True,
                                     stop=True).then_inc(list_mm, 1)
                if c == FULL_AT + 1:
                    pe.wait_ge(onehot_done, 2)
                    nc.tensor.matmul(list_ps2, expert_no[0:E, :], onehot_new[:], start=True,
                                     stop=True).then_inc(list_mm, 1)
            expert_pass(0, 1)
            expert_pass(NC_, 0)
            pe.wait_ge(tables_done, 1)
            last = pe.value_load(ends[0:1, 1:2], min_val=4 * NC_, max_val=2 * MAX_LOOPS * NC_)
            with pe.Fori(2 * NC_, last, 2 * NC_) as at:
                expert_pass(at, 1)
                expert_pass(at + NC_, 0)
            for c in range(NC_ + 3):
                if c < NC_:
                    gate_up(last, 1, c)
                if c < 2:
                    down(last, 1, c - 2)
                if 0 < c <= NC_:
                    float32_down(last, wd_raw, c - 1)
                if c >= 3:
                    transpose_out(c - 3)

        @block.vector
        def _(dve):
            v = nc.vector
            n = [0]

            def link(ins):
                n[0] += 1
                ins.then_inc(dve_step, 1)
                dve.wait_ge(dve_step, n[0])

            link(v.memset(ones[:], 1.0))
            v.memset(grp[:, :, GROUPS:], BIG)
            link(v.memset(masked[:, :, E:], BIG))

            def sum_stats(k, c):
                if k == 0:
                    dve.wait_ge(x_in[c], 16)
                else:
                    dve.wait_ge(x2_done, c + 1)
                for t in range(TPC):
                    ins = v.bn_stats(stats[k][:, t, :], x_all[:, TPC * c + t, :])
                ins.then_inc(stats_done[k], 1)

            def mean_variance(k, c):
                dve.wait_ge(stats_done[k], c + 1)
                for t in range(TPC):
                    ins = v.bn_aggr(mv[k][:, t, :], stats[k][:, t, :])
                ins.then_inc(mean_done[k], 1)

            def variance_eps(k, c):
                dve.wait_ge(mean_done[k], c + 1)
                wait(dve, xn_done[k], c)
                v.tensor_scalar(veps[k][:], mv[k][:, :, 1], EPS, None, ALU.add).then_inc(var_done[k], 1)

            def shifts(k, c):
                dve.wait_ge(rstd_done[k], c + 1)
                v.scalar_tensor_tensor(out=shift[k][:], in0=mv[k][:, :, 0], scalar=-1.0, in1=rstd[k][:],
                                       op0=ALU.mult, op1=ALU.mult).then_inc(shift_done[k], 1)

            def maxima(c, q):
                dve.wait_ge(s_mm, BPC * c + q + 1)
                wait(dve, probs_done, BPC * (c - 1) + q + 1)
                for r, w in enumerate((slice(0, P), slice(P, SW))):
                    ins = v.tensor_reduce(neg_max[:, 2 * q + r:2 * q + r + 1], attn_ps[q][:, w], AX_X, ALU.max,
                                          negate=True)
                ins.then_inc(max_done, 1)

            def sum_inverses(c):
                dve.wait_ge(probs_done, BPC * (c + 1))
                v.reciprocal(rsum[:], sums[:]).then_inc(rsum_done, 1)

            def residual(c):
                dve.wait_ge(rsum_done, c + 1)
                dve.wait_ge(o_mm, c + 1)
                for t in range(TPC):
                    ins = v.scalar_tensor_tensor(out=x_all[:, TPC * c + t, :], in0=o_ps[:, t * D:(t + 1) * D],
                                                 scalar=rsum[:, t:t + 1], in1=x_all[:, TPC * c + t, :],
                                                 op0=ALU.mult, op1=ALU.add)
                ins.then_inc(x2_done, 1)

            def route(c, step):
                if step == 0:
                    dve.wait_ge(logit_exp, c + 1)
                else:
                    dve.wait_ge(route_step, ROUTE_STEPS * c + step)
                sc = score[c % 2][:]
                if step == 0:
                    ins = v.tensor_scalar(sc, sc, 1.0, None, ALU.add)
                elif step == 1:
                    ins = v.reciprocal(sc, sc)
                elif step == 2:
                    if c == 0:
                        dve.wait_ge(weights_in, 16 * 3)
                    ins = v.tensor_tensor(sc, sc, bias_sb[:].unsqueeze(1).broadcast_to([P, TPC, E]), ALU.add)
                elif step == 3:
                    ins = v.tensor_reduce(grp[:, :, 0:GROUPS], sc.rearrange("p t (g e) -> p t g e", g=GROUPS),
                                          AX_X, ALU.max)
                elif step == 4:
                    for t in range(TPC):
                        ins = v.max(grp_top[:, t, :], grp[:, t, :])
                elif step == 5:
                    for t in range(TPC):
                        ins = v.match_replace(grp_rest[:, t, :], grp_top[:, t, :], grp[:, t, :], 2 * BIG)
                elif step == 6:
                    wait(dve, comb_done, c)
                    for t in range(TPC):
                        ins = v.scalar_tensor_tensor(
                            out=masked[:, t, 0:E].rearrange("p (g e) -> p g e", g=GROUPS),
                            in0=grp_rest[:, t, 0:GROUPS].unsqueeze(2).broadcast_to([P, GROUPS, GE]), scalar=2 * BIG,
                            in1=sc[:, t, :].rearrange("p (g e) -> p g e", g=GROUPS),
                            op0=ALU.is_equal, op1=ALU.mult)
                elif step == 7:
                    for t in range(TPC):
                        ins = v.max(top[:, t, :], masked[:, t, :])
                elif step == 8:
                    for t in range(TPC):
                        ins = v.match_replace(rest[:, t, :], top[:, t, :], masked[:, t, :], 0.0)
                elif step == 9:
                    ins = v.tensor_reduce(wsum[:], top[:, :, 8 - TOPK:], AX_X, ALU.add)
                elif step == 10:
                    ins = v.tensor_scalar(wsum[:], wsum[:], 1e-8, None, ALU.add)
                else:
                    v.reciprocal(wsum[:], wsum[:]).then_inc(picked, 1)
                    return
                ins.then_inc(route_step, 1)

            dve.wait_ge(expc_done, 1)
            link(v.tensor_scalar(silu_c[:], silu_c[:], 1.0, None, ALU.add))
            link(v.reciprocal(silu_c[:], silu_c[:]))
            v.tensor_tensor(silu_c[:], silu_c[:], cT_sb[:], ALU.mult).then_inc(siluc_done, 1)
            sum_stats(0, 0)
            mean_variance(0, 0)
            variance_eps(0, 0)
            shifts(0, 0)
            dve.wait_ge(mod_mm, 2)
            link(v.tensor_copy(modT[:].rearrange("p k b -> p (k b)"), bank[1][:, 0:NMOD * BATCH]))
            dve.sem_inc(mod_copied, 1)
            for k in (CA, CB):
                ins = v.tensor_scalar(modT[:, k, :], modT[:, k, :], 1.0, None, ALU.add)
            ins.then_inc(mod_ready, 1)
            v.tensor_copy(ga_row[:], bank[2][0:BATCH, 0:D]).then_inc(mod_copied, 1)
            dve.wait_ge(mod_copied, 2)

            def clamp(g, w):
                m = mod_tmp[0:g.shape[0], :, 0:w]
                v.tensor_scalar(m[:, 0, :], g, 0.0, None, ALU.is_ge)
                link(v.tensor_scalar(m[:, 1, :], g, 0.0, None, ALU.is_lt))
                v.scalar_tensor_tensor(out=m[:, 0, :], in0=g, scalar=0.25, in1=m[:, 0, :],
                                       op0=ALU.max, op1=ALU.mult)
                link(v.scalar_tensor_tensor(out=m[:, 1, :], in0=g, scalar=-0.25, in1=m[:, 1, :],
                                            op0=ALU.min, op1=ALU.mult))
                return v.tensor_tensor(g, m[:, 0, :], m[:, 1, :], ALU.add)

            link(clamp(ga_row[:], D))
            dve.sem_inc(ga_row_done, 1)
            link(clamp(modT[:, GB, :], BATCH))

            def split_pair(wd, u, n):
                v.tensor_copy(gu_hi[u][:], gu_raw[:])
                v.tensor_copy(wd_hi[u][:], wd[:]).then_inc(pair_high, NC_)
                dve.wait_ge(pair_high, NC_ * (n + 1))
                v.tensor_tensor(gu_lo[u][:], gu_raw[:], gu_hi[u][:], ALU.subtract)
                v.tensor_tensor(wd_lo[u][:], wd[:], wd_hi[u][:], ALU.subtract).then_inc(pair_split, NC_)

            def hidden_step(at, c):
                dve.wait_ge(weighted_done, at + (c + 1))
                dve.wait_ge(up_mm, steps(at, c))
                v.tensor_tensor(hidden[c % 2][:], up_ps[c % 2][:], weighted[c % 2][:], ALU.mult).then_inc(hidden_done, 1)

            def low_step(at, c):
                dve.wait_ge(high_done, split_steps(at, c))
                v.tensor_tensor(hid_lo[c % 2][:], hidden[c % 2][:], hid_hi[c % 2][:],
                                ALU.subtract).then_inc(low_done, 1)

            def sum_step(at, c):
                dve.wait_ge(down_mm, steps(at, c))
                a = acc[:, chunk_cols(c % NC_)]
                v.tensor_tensor(a, out_ps[c % 2][:], a, ALU.add).then_inc(acc_done, 1)

            def sums_pass(at):
                for c in range(NC_):
                    hidden_step(at, c)
                    sum_step(at, c - 2)
                    low_step(at, c)

            def finish(c):
                dve.wait_ge(yT_mm, c + 1)
                wait(dve, y_out[c % 2], 16 * (c // 2))
                v.tensor_tensor(y[c % 2][:].rearrange("p t d -> p (t d)"), t_ps[c % 2][:],
                                x_all[:, tiles(c), :].rearrange("p t d -> p (t d)"), ALU.add).then_inc(y_done, 1)

            for i in range(NC_ + 3):
                a, b, r, d = i + 1, i - 1, i - 3, i - 4
                has_a, has_b, has_r, has_d = (0 <= k < NC_ for k in (a, b, r, d))
                if has_b:
                    maxima(b, 0)
                if has_d:
                    route(d, 6)
                if has_b:
                    maxima(b, 1)
                if has_d:
                    route(d, 7)
                if has_a:
                    sum_stats(0, a)
                if has_d:
                    route(d, 8)
                if has_a:
                    mean_variance(0, a)
                if has_d:
                    route(d, 9)
                if has_a:
                    variance_eps(0, a)
                if has_d:
                    route(d, 10)
                if has_b:
                    sum_inverses(b)
                if has_d:
                    route(d, 11)
                if i == 1:
                    v.memset(acc[:, FP32_STEPS * CT:], 0.0)
                    dve.wait_ge(shared_in, 16 * 4)
                    split_pair(wd_shared, 0, 0)
                if has_r:
                    route(r, 0)
                if has_a:
                    shifts(0, a)
                if has_r:
                    route(r, 1)
                if has_b:
                    residual(b)
                if has_r:
                    route(r, 2)
                if has_b:
                    sum_stats(1, b)
                if has_r:
                    route(r, 3)
                if has_b:
                    mean_variance(1, b)
                    variance_eps(1, b)
                if has_r:
                    route(r, 4)
                    route(r, 5)
                if has_b:
                    shifts(1, b)

            c = NC_ - 1
            dve.wait_ge(combT_done, c)
            v.tensor_reduce(act_any[:, 0:1], comb_sum[:, 0:c], AX_X, ALU.max).then_inc(act_any_done, 1)
            route(c, 6)
            dve.wait_ge(act_any_done, 1)
            v.tensor_scalar(act[:, 0:1], act_any[:, 0:1], 0.0, None, ALU.is_gt).then_inc(act_done, 1)
            route(c, 7)
            dve.wait_ge(pos_mm, 1)
            v.tensor_scalar(base[:], count_ps1, 2.0, None, ALU.max)
            link(v.tensor_copy(pos[:, 0:1], place_ps1))
            v.tensor_scalar(onehot[:], place_no[0:E, :], pos[:, 0:1], act[:, 0:1], ALU.is_equal,
                            ALU.mult).then_inc(onehot_done, 1)
            route(c, 8)
            route(c, 9)
            route(c, 10)
            route(c, 11)
            dve.wait_ge(picked, NC_)
            dve.wait_ge(combT_mm, NC_ - 1)
            v.tensor_tensor(comb[:], masked[:, :, 0:E], rest[:, :, 0:E], ALU.subtract).then_inc(chosen_done, 1)
            dve.wait_ge(list_mm, 1)
            v.tensor_scalar(first_pair[:], list_ps1, float(E), None, ALU.add).then_inc(pair_known, 1)
            dve.wait_ge(chosen_done, NC_)
            v.tensor_tensor(comb[:], comb[:], wsum[:].unsqueeze(2).broadcast_to([P, TPC, E]),
                            ALU.mult).then_inc(comb_done, 1)
            dve.wait_ge(combT_done, NC_)
            link(v.tensor_tensor(act_any[:, 1:2], act_any[:, 0:1], comb_sum[:, c:c + 1], ALU.max))
            link(v.tensor_scalar(act[:, 1:2], act_any[:, 1:2], 0.0, None, ALU.is_gt))
            v.tensor_tensor(new[:], act[:, 1:2], act[:, 0:1], ALU.subtract).then_inc(act_done, 1)
            dve.wait_ge(pos_mm, 2)
            v.tensor_tensor(n_act[:], count_ps2, base[0:1, :], ALU.add)
            link(v.tensor_tensor(pos[:, 1:2], place_ps2, base[:], ALU.add))
            link(v.tensor_scalar(onehot_new[:], place_no[0:E, :], pos[:, 1:2], new[:], ALU.is_equal, ALU.mult))
            v.tensor_tensor(onehot_new[:], onehot_new[:], onehot[:], ALU.add).then_inc(onehot_done, 1)
            link(v.tensor_scalar(before[:], loop_start[:], n_act[:], None, ALU.is_lt))
            link(v.tensor_reduce(n_loops[:], before[:], AX_X, ALU.add))
            link(v.tensor_scalar(n_loops[:], n_loops[:], 2.0, None, ALU.max))
            v.tensor_scalar(ends[:, 0:1], n_loops[:], 2.0, None, ALU.mult)
            v.tensor_scalar(ends[:, 1:2], n_loops[:], 2.0 * NC_, None, ALU.mult)
            dve.wait_ge(pair_in, 64)
            split_pair(wd_raw, 1, 1)
            dve.wait_ge(list_mm, 2)
            link(v.tensor_scalar(lists[:], list_ps2, float(E), None, ALU.add))
            dve.sem_inc(tables_done, 1)
            low_step(-NC_, FP32_STEPS)
            low_step(-NC_, NC_ - 1)
            dve.wait_ge(hidden_done, NC_)
            dve.wait_ge(acc_done, FP32_STEPS)
            dve.wait_ge(low_done, NC_ - FP32_STEPS)

            sums_pass(0)
            sums_pass(NC_)
            last = dve.value_load(ends[0:1, 1:2], min_val=4 * NC_, max_val=2 * MAX_LOOPS * NC_)
            with dve.Fori(2 * NC_, last, 2 * NC_) as at:
                sums_pass(at)
                sums_pass(at + NC_)
            for c in range(NC_ + 3):
                if c == 1:
                    dve.wait_ge(low_done, split_steps(last, -1))
                if c < NC_:
                    hidden_step(last, c)
                if c < 2:
                    sum_step(last, c - 2)
                if 0 < c <= NC_:
                    sum_step(last, c - 1)
                if c >= 3:
                    finish(c - 3)


_OUT = "out"


def kernel(**inputs):
    import numpy as np
    import concourse.bacc as bacc
    from concourse.bass_utils import run_bass_kernel_spmd as run

    a = {k[3:]: np.asarray(v) for k, v in inputs.items()}
    sh = lambda w: w.reshape(NSH, INTER, D)
    gates = np.concatenate([a["ffn_eg_w"], sh(a["ffn_sg_w"])])
    ups = np.concatenate([a["ffn_eu_w"], sh(a["ffn_su_w"])])
    downs = np.concatenate([a["ffn_ed_w"], a["ffn_sd_w"].reshape(D, NSH, INTER).transpose(1, 0, 2)])
    arrays = {
        "x": a["attn_x"],
        "cT": a["c"].T,
        "wmod": a["wmod"],
        "wqT": a["attn_Wq"].T,
        "wkT": a["attn_Wk"].T,
        "wv": a["attn_Wv"],
        "gate_wT": a["ffn_gate_w"].T,
        "gate_bias": a["ffn_gate_bias"],
        "w_gu": np.concatenate([gates, ups], axis=1).transpose(0, 2, 1),
        "w_down": downs.transpose(0, 2, 1),
    }
    arrays = {k: np.ascontiguousarray(v) for k, v in arrays.items()}
    nc = bacc.Bacc("TRN2", target_bir_lowering=False, num_devices=1)
    args = [nc.dram_tensor(k, v.shape, mybir.dt.from_np(v.dtype), kind="ExternalInput").ap()
            for k, v in arrays.items()]
    args.append(nc.dram_tensor("ga_dram", [BATCH, D], F32).ap())
    args.append(nc.dram_tensor("comb_dram", [E + 1, TOKENS], F32).ap())
    args.append(nc.dram_tensor(_OUT, (BATCH, SEQ, D), F32, kind="ExternalOutput").ap())
    build(nc, *args)
    r = run(nc, [arrays], core_ids=[0])
    return r.results[0][_OUT]
```
